# Optimizing a Trainium2 kernel written in Bass

```python
import numpy as np
import jax
import jax.numpy as jnp

def _softmax(x, axis=-1):
    return jax.nn.softmax(x, axis=axis)

def _gelu(x):
    return jax.nn.gelu(x, approximate=True)

def _silu(x):
    return jax.nn.silu(x)

def _sigmoid(x):
    return jax.nn.sigmoid(x)

def _layernorm(x, axis=-1, eps=1e-05):
    m = jnp.mean(x, axis=axis, keepdims=True)
    v = jnp.var(x, axis=axis, keepdims=True)
    return (x - m) / jnp.sqrt(v + eps)

def _scatter_add(tgt, idx, src, axis=0):
    return tgt.at[idx].add(src)

def _segment_sum(src, seg, n):
    return jax.ops.segment_sum(src, seg, n)
kernel_name = 'mk_recurrent_d1_jaxref_r8_49a0fe'

def setup_inputs(seed: int=0):
    np.random.seed(seed)
    _w = jnp.asarray

    def _L0_attn_setup():
        import jax, jax.numpy as jnp
        import numpy as np
        EMBED = 128
        HEADS = 16
        SPARSITY = 4
        B, S = (2, 256)

        def _mask(seq_len):
            i = jnp.arange(seq_len)[:, None]
            j = jnp.arange(seq_len)[None, :]
            upper = j > i
            return upper | upper & ((j - i) % SPARSITY != 0)
        key = jax.random.key(seed)
        k0, k1, k2, k3, k4 = jax.random.split(key, 5)
        E = EMBED
        x = jax.random.normal(k0, (B, S, E), jnp.float32)
        in_proj_w = jax.random.normal(k1, (3 * E, E), jnp.float32) * E ** (-0.5)
        in_proj_b = jax.random.normal(k2, (3 * E,), jnp.float32) * 0.02
        out_proj_w = jax.random.normal(k3, (E, E), jnp.float32) * E ** (-0.5)
        out_proj_b = jax.random.normal(k4, (E,), jnp.float32) * 0.02
        return {'x': x, 'in_proj_w': in_proj_w, 'in_proj_b': in_proj_b, 'out_proj_w': out_proj_w, 'out_proj_b': out_proj_b}
    _L0_attn_in = _L0_attn_setup()

    def _L0_ffn_setup():
        import jax, jax.numpy as jnp
        import numpy as np
        from jax import lax
        B, L, D, E, K, DFF = (4, 256, 128, 8, 2, 256)
        key = jax.random.key(seed)
        k1, k2, k3, k4, k5 = jax.random.split(key, 5)
        s = 0.02
        return {'x': jax.random.normal(k1, (B, L, D), dtype=jnp.float32), 'Wr': jax.random.normal(k2, (D, E), dtype=jnp.float32) * s, 'Wg': jax.random.normal(k3, (E, D, DFF), dtype=jnp.float32) * s, 'Wu': jax.random.normal(k4, (E, D, DFF), dtype=jnp.float32) * s, 'Wd': jax.random.normal(k5, (E, DFF, D), dtype=jnp.float32) * s}
    _L0_ffn_in = _L0_ffn_setup()
    _d = {'L0_attn_x': _L0_attn_in['x'], 'L0_attn_in_proj_w': _L0_attn_in['in_proj_w'], 'L0_attn_in_proj_b': _L0_attn_in['in_proj_b'], 'L0_attn_out_proj_w': _L0_attn_in['out_proj_w'], 'L0_attn_out_proj_b': _L0_attn_in['out_proj_b'], 'L0_ffn_Wr': _L0_ffn_in['Wr'], 'L0_ffn_Wg': _L0_ffn_in['Wg'], 'L0_ffn_Wu': _L0_ffn_in['Wu'], 'L0_ffn_Wd': _L0_ffn_in['Wd']}
    _x0 = _d['L0_attn_x']
    _d['L0_attn_x'] = jax.random.normal(jax.random.fold_in(jax.random.key(seed), 1), (2, 1024, 128), dtype=_x0.dtype)
    del _x0
    return _d

def reference(L0_attn_x, L0_attn_in_proj_w, L0_attn_in_proj_b, L0_attn_out_proj_w, L0_attn_out_proj_b, L0_ffn_Wr, L0_ffn_Wg, L0_ffn_Wu, L0_ffn_Wd):

    def _L0_attn_ref(x, in_proj_w, in_proj_b, out_proj_w, out_proj_b):
        import jax, jax.numpy as jnp
        import numpy as np
        EMBED = 128
        HEADS = 16
        SPARSITY = 4
        B, S = (2, 256)

        def _mask(seq_len):
            i = jnp.arange(seq_len)[:, None]
            j = jnp.arange(seq_len)[None, :]
            upper = j > i
            return upper | upper & ((j - i) % SPARSITY != 0)
        b, s, e = x.shape
        h = HEADS
        d = e // h
        qkv = x @ in_proj_w.T + in_proj_b
        q, k, v = jnp.split(qkv, 3, axis=-1)
        q = q.reshape(b, s, h, d)
        k = k.reshape(b, s, h, d)
        v = v.reshape(b, s, h, d)
        scores = jnp.einsum('bqhd,bkhd->bhqk', q, k) * d ** (-0.5)
        scores = jnp.where(_mask(s)[None, None], -jnp.inf, scores)
        attn = jax.nn.softmax(scores, axis=-1)
        ctx = jnp.einsum('bhqk,bkhd->bqhd', attn, v).reshape(b, s, e)
        return ctx @ out_proj_w.T + out_proj_b

    def _L0_ffn_ref(x, Wr, Wg, Wu, Wd):
        import jax, jax.numpy as jnp
        import numpy as np
        from jax import lax
        B, L, D, E, K, DFF = (4, 256, 128, 8, 2, 256)
        Bq, Lq, Dq = x.shape
        T = Bq * Lq
        xf = x.reshape(T, Dq)
        probs = jax.nn.softmax(xf @ Wr, axis=-1)
        k_vals, k_ids = lax.top_k(probs, K)
        k_w = k_vals / jnp.sum(k_vals, axis=-1, keepdims=True)
        combine = jnp.zeros((T, probs.shape[-1]), dtype=x.dtype)
        combine = combine.at[jnp.arange(T)[:, None], k_ids].add(k_w)

        def step(acc, params):
            wg, wu, wd, ce = params
            h = jax.nn.relu(xf @ wg) * (xf @ wu)
            return (acc + ce[:, None] * (h @ wd), None)
        acc0 = jnp.zeros((T, Dq), dtype=x.dtype)
        out, _ = lax.scan(step, acc0, (Wg, Wu, Wd, combine.T))
        return out.reshape(Bq, Lq, Dq)
    x = L0_attn_x
    xn = _layernorm(x, axis=-1)
    s = _L0_attn_ref(xn, L0_attn_in_proj_w, L0_attn_in_proj_b, L0_attn_out_proj_w, L0_attn_out_proj_b)
    g = _silu(_L0_ffn_ref(xn, L0_ffn_Wr, L0_ffn_Wg, L0_ffn_Wu, L0_ffn_Wd))
    x = x + s * g
    return x

_drawn_inputs = setup_inputs


def setup_inputs(seed=0):
    import zlib

    import numpy as np

    out = dict(_drawn_inputs(seed))
    spreads = {}
    factors = {'L0_attn_in_proj_w': 8.0,
     'L0_attn_in_proj_b': 8.0,
     'L0_attn_out_proj_w': 8.0,
     'L0_attn_out_proj_b': 182.482,
     'L0_ffn_Wr': 8.0,
     'L0_ffn_Wg': 8.0,
     'L0_ffn_Wu': 8.0,
     'L0_ffn_Wd': 8.0}
    for name, (base, spread) in spreads.items():
        noise = np.random.default_rng([zlib.crc32(name.encode()), seed]).standard_normal(out[name].shape)
        drawn = base * np.exp(spread * noise) if base else spread * noise
        out[name] = jnp.asarray(drawn.astype(out[name].dtype))
    for name, factor in factors.items():
        out[name] = (out[name] * factor).astype(out[name].dtype)
    return out
```

```python
from contextlib import ExitStack

import concourse.bass as bass
from concourse import mybir

F32 = mybir.dt.float32
BF16 = mybir.dt.bfloat16
ALU = mybir.AluOpType
ACT = mybir.ActivationFunctionType
X = mybir.AxisListType.X

P = 128
B, S, E = 2, 1024, 128
H, D = 16, 8
G = 4
PAIRS = G // 2
UNITS = B * H // G
TILES = B * S // P
QB = S // P
CH = 512
EXPERTS, DFF = 8, 256
FC = DFF // P
TOK = B * S // UNITS
Q_PARTS = (0, 0, 0, 1, 1, 2)
K_PARTS = (0, 1, 2, 0, 1, 0)
NT = len(Q_PARTS)
ROWS = NT * D
HALF = P // 2
SLOT = 32
SCALE = float(D) ** -0.5
EPS = 1e-5
MASKED = -1e30

A_TILES = [(qb, kc, pr) for qb in range(QB) for kc in range(qb * P // CH + 1) for pr in range(PAIRS)]
B_STEPS = [(qc, kb) for qc in range(S // CH) for kb in range((qc + 1) * CH // P)]
NA, NB = len(A_TILES), len(B_STEPS)
CHUNKS = S // CH
LAST_STEP = [max(i for i, (q, _) in enumerate(B_STEPS) if q == qc) for qc in range(CHUNKS)]
NC = EXPERTS * FC
A_SLOTS = 12
A_PER = NA // A_SLOTS
M_STEPS, SILU_STEPS, CTX_STEPS = 5, 3, 2
M_COLS = 2 * 3 * PAIRS * QB


def build(nc, x, w_in, b_in, b_in_row, w_out, b_out, w_router, w_gate, w_up, w_down, out):
    q_scr = nc.dram_tensor("q_scratch", (B, P, NT, S), BF16).ap()
    k_scr = nc.dram_tensor("k_scratch", (B, P, NT, S), BF16).ap()
    ce_scr = nc.dram_tensor("combine_scratch", (EXPERTS, B * S), F32).ap()

    ctx = ExitStack()
    with ctx:
        def sb(name, shape, dt=F32):
            return ctx.enter_context(nc.sbuf_tensor(name, shape, dt))

        def sem(name):
            return ctx.enter_context(nc.semaphore(name))

        ps = ctx.enter_context(nc.psum_tensor("ps", [P, 8, CH], F32))

        x_sb = sb("x_sb", [P, TILES, E])
        xn_t = sb("xn_t", [P, B * S])
        w_in_sb = sb("w_in_sb", [P, 3 * E])
        w_out_sb = sb("w_out_sb", [P, E])
        b_qk = sb("b_qk", [P, 2])
        b_v = sb("b_v", [P, E])
        b_o = sb("b_o", [P, 1])
        wr_sb = sb("wr_sb", [P, EXPERTS])
        wg_sb = sb("wg_sb", [P, EXPERTS, DFF])
        wu_sb = sb("wu_sb", [P, EXPERTS, DFF])
        wd_sb = sb("wd_sb", [P, EXPERTS * FC, E])
        ident = sb("ident", [P, P])
        ident_h = sb("ident_h", [P, P], BF16)
        mask_q = sb("mask_q", [P, P], BF16)
        mask_k = sb("mask_k", [P, P], BF16)
        rank = sb("rank", [P, EXPERTS])
        ones_rows = sb("ones_rows", [3, 2 * S], BF16)
        q_a = sb("q_a", [P, PAIRS, S], BF16)
        k_a = sb("k_a", [P, PAIRS, 2, S], BF16)
        q_b = sb("q_b", [P, PAIRS, S], BF16)
        k_b = sb("k_b", [P, PAIRS, 2, S], BF16)
        v_all = sb("v_all", [P, UNITS, QB, G, SLOT])
        v_b = sb("v_b", [P, QB, G, SLOT])
        ce_b = sb("ce_b", [P, EXPERTS, TOK])
        x_cur = sb("x_cur", [P, TOK])
        x_ce = sb("x_ce", [P, EXPERTS, TOK])
        gate = sb("gate", [P, 2, TOK])
        hid = sb("hid", [P, 2, TOK])
        probs = sb("probs", [P, 2, G, CH])
        mx = sb("mx", [P, CHUNKS, 2, PAIRS, QB])
        neg_m = sb("neg_m", [P, 2, PAIRS, QB])
        m_rest = sb("m_rest", [P, 2, 2, PAIRS, QB])
        m_parts = sb("m_parts", [P, 2, 3, PAIRS, QB], BF16)
        m_t = sb("m_t", [M_COLS, P], BF16)
        raw_t = sb("raw_t", [P, CH])
        rsum = sb("rsum", [P, 4, G])
        ctx_n = sb("ctx_n", [P, UNITS, QB, G * D])
        ctx_row = sb("ctx_row", [P, TILES, E])
        silu_b = sb("silu_b", [P, 3, TOK])
        g_t = sb("g_t", [P, B * S])
        parts = sb("parts", [P, 2, 3, S], BF16)
        rest = sb("rest", [P, 2, S])
        stat = sb("stat", [P, 8, TILES])
        rt = sb("rt", [P, 12, TILES, EXPERTS])
        rs = sb("rs", [P, 8, TILES])
        ce_t = sb("ce_t", [P, P])
        last = x_ce[:, :, :].rearrange("p (a b) t -> p a (b t)", a=4)
        ctx_t, y_t = last[:, 0:2, :], last[:, 2:4, :]
        o_sb = ce_b[:, 0:4, :].rearrange("p (a b) t -> p a (b t)", a=2)

        x_loaded = [sem(f"x_loaded{b}") for b in range(B)]
        proj_loaded = sem("proj_loaded")
        ffn_loaded = sem("ffn_loaded")
        consts_ready = sem("consts_ready")
        pool_step = sem("pool_step")
        ones_ready = sem("ones_ready")
        ones_placed = sem("ones_placed")
        centred = sem("centred")
        squared = sem("squared")
        var_ready = sem("var_ready")
        sd_ready = sem("sd_ready")
        dve_step = sem("dve_step")
        xn_ready = sem("xn_ready")
        xn_turned = sem("xn_turned")
        xnt_ready = sem("xnt_ready")
        qk_done = sem("qk_done")
        v_done = sem("v_done")
        high_ready = sem("high_ready")
        rest_ready = sem("rest_ready")
        mid_ready = sem("mid_ready")
        low_ready = sem("low_ready")
        v_ready = sem("v_ready")
        scr_written = sem("scr_written")
        logits_done = sem("logits_done")
        logits_cut = sem("logits_cut")
        router_exp = sem("router_exp")
        combine_ready = sem("combine_ready")
        combine_turned = sem("combine_turned")
        combine_copied = sem("combine_copied")
        combine_written = sem("combine_written")
        a_loaded = sem("a_loaded")
        b_loaded = sem("b_loaded")
        m_loaded = sem("m_loaded")
        ce_loaded = sem("ce_loaded")
        xcur_ready = sem("xcur_ready")
        a_scored = sem("a_scored")
        a_reduced = sem("a_reduced")
        m_step = sem("m_step")
        m_turned = sem("m_turned")
        m_copied = sem("m_copied")
        gu_done = sem("gu_done")
        relu_done = sem("relu_done")
        hid_ready = sem("hid_ready")
        ffn_done = sem("ffn_done")
        ez_done = sem("ez_done")
        silu_step = sem("silu_step")
        b_scored = sem("b_scored")
        exp_done = sem("exp_done")
        pv_done = sem("pv_done")
        raw_copied = sem("raw_copied")
        raw_turned = sem("raw_turned")
        ctx_step = sem("ctx_step")
        ctx_gathered = sem("ctx_gathered")
        ctx_turned = sem("ctx_turned")
        ctxt_ready = sem("ctxt_ready")
        proj_done = sem("proj_done")
        y_ready = sem("y_ready")
        y_turned = sem("y_turned")
        o_ready = sem("o_ready")
        stored = [sem(f"stored{i}") for i in range(2)]

        block = ctx.enter_context(nc.Block())

        def span_a(i):
            qb, kc, _ = A_TILES[i]
            w = min(CH, (qb + 1) * P - kc * CH)
            return w, kc == qb * P // CH

        def span_b(i):
            qc, kb = B_STEPS[i]
            q0 = max(qc * CH, kb * P)
            return q0, (qc + 1) * CH - q0, kb * P >= qc * CH

        @block.sync
        def _(sp):
            xv = x.rearrange("b (t p) e -> b p t e", p=P)
            for b in range(B):
                sp.dma_start(x_sb[:, b * QB:(b + 1) * QB, :], xv[b]).then_inc(x_loaded[b], 16)
            sp.dma_start(w_in_sb[:, :], w_in).then_inc(proj_loaded, 16)
            sp.dma_start(b_qk[:, :], b_in[:, 0:2]).then_inc(proj_loaded, 16)
            sp.dma_start(b_v[:, :], b_in_row[:, 2 * E:3 * E].to_broadcast([P, E])).then_inc(proj_loaded, 16)
            sp.dma_start(wr_sb[:, :], w_router).then_inc(proj_loaded, 16)
            sp.dma_start(wg_sb[:, :, :], w_gate.rearrange("e d f -> d e f")).then_inc(ffn_loaded, 16)
            sp.dma_start(wu_sb[:, :, :], w_up.rearrange("e d f -> d e f")).then_inc(ffn_loaded, 16)
            sp.dma_start(wd_sb[:, :, :], w_down.rearrange("e (c f) d -> f (e c) d", f=P)).then_inc(ffn_loaded, 16)
            sp.dma_start(w_out_sb[:, :], w_out).then_inc(ffn_loaded, 16)
            sp.dma_start(b_o[:, :], b_out).then_inc(ffn_loaded, 16)
            sp.wait_ge(ones_ready, 2)
            for hh in range(2):
                r = hh * HALF + ROWS
                sp.dma_start(k_b[r:r + 3, :, hh, :], ones_rows[:, :].rearrange("r (a s) -> r a s", a=2))\
                  .then_inc(ones_placed, 16)
            for b in range(B):
                for i, (scr, parts_of) in enumerate(((q_scr, Q_PARTS), (k_scr, K_PARTS))):
                    sp.wait_ge(high_ready, 2 * b + i + 1)
                    sp.wait_ge(mid_ready, 2 * b + i + 1)
                    sp.wait_ge(low_ready, 2 * b + i + 1)
                    for t, part in enumerate(parts_of):
                        sp.dma_start(scr[b, :, t, :], parts[:, i, part, :]).then_inc(scr_written, 16)
                sp.wait_ge(scr_written, 16 * 2 * NT * (b + 1))

            q_u = q_scr.rearrange("b (g a c d) t s -> (b g) c (d t) a s", g=H // G, a=PAIRS, c=2)
            k_u = k_scr.rearrange("b (g a c d) t s -> (b g) c (d t) a s", g=H // G, a=PAIRS, c=2)

            def load_qk(q_to, k_to, n, done):
                for hh in range(2):
                    r = slice(hh * HALF, hh * HALF + ROWS)
                    sp.dma_start(q_to[r, :, :], q_u[n, hh]).then_inc(done, 16)
                    sp.dma_start(k_to[r, :, hh, :], k_u[n, hh]).then_inc(done, 16)

            def load_ce(n):
                src = ce_scr[:, bass.ts(n, TOK)].unsqueeze(0).to_broadcast([P, EXPERTS, TOK])
                sp.dma_start(ce_b[:, :, :], src).then_inc(ce_loaded, 16)

            def load_b(n):
                load_qk(q_b, k_b, n, b_loaded)
                sp.dma_start(v_b[:, :, :, :].rearrange("p k g s -> p (k g s)"),
                             v_flat[:, bass.ts(n, QB * G * SLOT)]).then_inc(b_loaded, 16)

            def load_m(n):
                sp.wait_ge(m_copied, n + 1)
                for hh in range(2):
                    r = hh * HALF + ROWS
                    sp.dma_start(q_b[r:r + 3, :, :].rearrange("r a (b q) -> r a b q", q=P),
                                 m_t[hh * M_COLS // 2:(hh + 1) * M_COLS // 2, :]).then_inc(m_loaded, 16)

            v_flat = v_all[:, :, :, :, :].rearrange("p u k g s -> p (u k g s)")
            sp.wait_ge(consts_ready, 1)
            load_qk(q_a, k_a, 0, a_loaded)
            sp.wait_ge(v_ready, B * QB // 2)
            load_b(0)
            sp.wait_ge(combine_copied, 1)
            sp.dma_start(ce_scr.rearrange("e (t k) -> (e t) k", k=P), ce_t[:, :]).then_inc(combine_written, 16)
            sp.wait_ge(combine_written, 16)
            load_ce(0)
            load_m(0)
            with sp.Fori(1, UNITS) as n:
                sp.wait_ge(a_scored, n * NA)
                load_qk(q_a, k_a, n, a_loaded)
                sp.wait_ge(xcur_ready, n * (EXPERTS + 1))
                load_ce(n)
                sp.wait_ge(pv_done, n * NB)
                load_b(n)
                load_m(n)
            ov = out.rearrange("b (t p) e -> p (b t) e", p=P)
            for c in range(B * CHUNKS):
                sp.wait_ge(o_ready, c + 1)
                sp.dma_start(ov[:, 4 * c:4 * c + 4, :], o_sb[:, c % 2, :].rearrange("p (t e) -> p t e", e=E))\
                  .then_inc(stored[c % 2], 16)
            for i in range(2):
                sp.wait_ge(stored[i], 16 * B * CHUNKS // 2)

        @block.gpsimd
        def _(pool):
            steps = [0]

            def link(ins):
                steps[0] += 1
                ins.then_inc(pool_step, 1)
                pool.wait_ge(pool_step, steps[0])

            nc.gpsimd.memset(ident[:, :], 0.0)
            nc.gpsimd.memset(ident_h[:, :], 0.0)
            nc.gpsimd.memset(mask_q[:, :], 0.0)
            nc.gpsimd.memset(mask_k[:, :], 0.0)
            nc.gpsimd.memset(ones_rows[:, :], 1.0).then_inc(ones_ready, 1)
            for e in range(EXPERTS):
                link(nc.gpsimd.memset(rank[:, e:e + 1], float(EXPERTS - e)))
            for m in (ident, ident_h):
                nc.gpsimd.affine_select(out=m[:, :], in_=m[:, :], compare_op=ALU.not_equal, fill=1.0, base=0,
                                        pattern=[[-1, P]], channel_multiplier=1)
            nc.gpsimd.affine_select(out=mask_q[:, :], in_=mask_q[:, :], compare_op=ALU.is_ge, fill=MASKED, base=0,
                                    pattern=[[-1, P]], channel_multiplier=1)
            link(nc.gpsimd.affine_select(out=mask_k[:, :], in_=mask_k[:, :], compare_op=ALU.is_ge, fill=MASKED,
                                         base=0, pattern=[[1, P]], channel_multiplier=-1))
            nc.gpsimd.memset(k_b[:, :, :, :].bitcast(F32), 0.0)
            nc.gpsimd.memset(q_b[:, :, :].bitcast(F32), 0.0).then_inc(ones_ready, 1)
            nc.gpsimd.memset(k_a[:, :, :, :].bitcast(F32), 0.0)
            nc.gpsimd.memset(q_a[:, :, :].bitcast(F32), 0.0).then_inc(consts_ready, 1)

            for b in range(B):
                for i in range(2):
                    pool.wait_ge(rest_ready, 2 * b + i + 1)
                    if b:
                        pool.wait_ge(scr_written, 16 * 2 * NT * b)
                    nc.gpsimd.tensor_copy(parts[:, i, 1, :], rest[:, i, :]).then_inc(mid_ready, 1)
                    pool.wait_ge(mid_ready, 2 * b + i + 1)
                    nc.gpsimd.tensor_tensor(parts[:, i, 2, :], rest[:, i, :], parts[:, i, 1, :], ALU.subtract)\
                      .then_inc(low_ready, 1)

            def inputs(n):
                tok = xn_t[:, bass.ts(n, TOK)]
                nc.gpsimd.tensor_copy(x_cur[:, :], tok).then_inc(xcur_ready, 1)
                for e in range(EXPERTS):
                    nc.gpsimd.tensor_tensor(x_ce[:, e, :], tok, ce_b[:, e, :], ALU.mult).then_inc(xcur_ready, 1)

            pool.wait_ge(xnt_ready, 1)
            pool.wait_ge(ce_loaded, 16)
            inputs(0)
            with pool.Fori(1, UNITS) as n:
                pool.wait_ge(gu_done, n * NC)
                pool.wait_ge(ce_loaded, n * 16 + 16)
                inputs(n)
            for c in range(B * CHUNKS):
                b, t0 = c // CHUNKS, (c % CHUNKS) * 4
                pool.wait_ge(ctx_step, (b * (H // G) * CHUNKS + (H // G - 1) * CHUNKS + c % CHUNKS + 1) * CTX_STEPS)
                nc.gpsimd.tensor_copy(
                    ctx_row[:, 4 * c:4 * c + 4, :].rearrange("p t (g e) -> p t g e", g=H // G),
                    ctx_n[:, b * (H // G):(b + 1) * (H // G), t0:t0 + 4, :].rearrange("p g t e -> p t g e"))\
                  .then_inc(ctx_gathered, 1)

        @block.scalar
        def _(act):
            sq = probs[:, :, :, :].rearrange("p a g c -> p (a g c)")
            for b in range(B):
                act.wait_ge(centred, b + 1)
                nc.scalar.activation(sq[:, 2048 + b * 1024:2048 + (b + 1) * 1024],
                                     sq[:, b * 1024:(b + 1) * 1024], ACT.Square).then_inc(squared, 1)
                act.wait_ge(var_ready, b + 1)
                nc.scalar.activation(stat[:, 2, b * QB:(b + 1) * QB], stat[:, 1, b * QB:(b + 1) * QB], ACT.Sqrt)\
                  .then_inc(sd_ready, 1)
            for b in range(B):
                act.wait_ge(xn_turned, b + 1)
                nc.scalar.activation(xn_t[:, b * S:(b + 1) * S], ps[:, 0:2, :].rearrange("p a c -> p (a c)"),
                                     ACT.Copy).then_inc(xnt_ready, 1)
                for i in range(2):
                    act.wait_ge(qk_done, 2 * b + i + 1)
                    if b:
                        act.wait_ge(scr_written, 16 * 2 * NT * b)
                    if b == 0 and i == 0:
                        act.wait_ge(proj_loaded, 64)
                    nc.scalar.activation(parts[:, i, 0, :],
                                         ps[:, 2 + 2 * i:4 + 2 * i, :].rearrange("p a c -> p (a c)"),
                                         ACT.Identity, bias=b_qk[:, i:i + 1]).then_inc(high_ready, 1)
            act.wait_ge(logits_cut, 1)
            nc.scalar.activation(rt[:, 1, :, :], rt[:, 0, :, :], ACT.Exp).then_inc(router_exp, 1)
            act.wait_ge(combine_turned, 1)
            nc.scalar.activation(ce_t[:, :], ps[:, 1, 0:P], ACT.Copy).then_inc(combine_copied, 1)

            def feed_forward(n):
                for s in range(NC):
                    act.wait_ge(gu_done, n * NC + s + 1)
                    nc.scalar.activation(gate[:, s % 2, :], ps[:, 4 + s % 2, 0:TOK], ACT.Relu)\
                      .then_inc(relu_done, 1)
                    if s == A_SLOTS + 1:
                        act.wait_ge(m_turned, n + 1)
                        nc.scalar.activation(m_t[:, :], ps[0:M_COLS, 6, 0:P // 2].bitcast(BF16), ACT.Copy)\
                          .then_inc(m_copied, 1)
                act.wait_ge(ffn_done, n + 1)
                nc.scalar.activation(silu_b[:, 0, :], ps[:, 7, 0:TOK], ACT.Exp, scale=-1.0).then_inc(ez_done, 1)

            def exps(n):
                for s in range(NB):
                    _, w, _ = span_b(s)
                    for pr in range(PAIRS):
                        i = s * PAIRS + pr
                        act.wait_ge(b_scored, n * NB * PAIRS + i + 1)
                        k = 2 * (i % 3)
                        nc.scalar.activation(probs[:, s % 2, 2 * pr:2 * pr + 2, 0:w], ps[:, k:k + 2, 0:w],
                                             ACT.Exp, scale=SCALE).then_inc(exp_done, 1)

            feed_forward(0)
            with act.Fori(1, UNITS) as n:
                exps(n - 1)
                feed_forward(n)
            exps(UNITS - 1)
            for c in range(B * CHUNKS):
                act.wait_ge(ctx_turned, c + 1)
                if c >= 2:
                    act.wait_ge(proj_done, c - 1)
                nc.scalar.activation(ctx_t[:, c % 2, :], ps[:, 4 * (c % 2), :], ACT.Copy).then_inc(ctxt_ready, 1)

        @block.vector
        def _(dve):
            steps = [0]

            def link(ins):
                steps[0] += 1
                ins.then_inc(dve_step, 1)
                dve.wait_ge(dve_step, steps[0])

            sq = probs[:, :, :, :].rearrange("p a g c -> p (a g c)")
            nc.vector.memset(mx[:, :, :, :, :], 4 * MASKED)
            link(nc.vector.memset(v_all[:, :, :, :, :], 0.0))
            link(nc.vector.memset(v_all[:, :, :, :, D:D + 1], 1.0))
            for b in range(B):
                t = slice(b * QB, (b + 1) * QB)
                xcb = sq[:, b * 1024:(b + 1) * 1024].rearrange("p (t e) -> p t e", e=E)
                xsq = sq[:, 2048 + b * 1024:2048 + (b + 1) * 1024].rearrange("p (t e) -> p t e", e=E)
                dve.wait_ge(x_loaded[b], 16)
                link(nc.vector.tensor_reduce(stat[:, 0, t], x_sb[:, t, :], X, ALU.add))
                link(nc.vector.tensor_scalar(stat[:, 0, t], stat[:, 0, t], 1.0 / E, None, ALU.mult))
                nc.vector.tensor_tensor(xcb, x_sb[:, t, :], stat[:, 0, t].unsqueeze(2).to_broadcast([P, QB, E]),
                                        ALU.subtract).then_inc(centred, 1)
                dve.wait_ge(squared, b + 1)
                link(nc.vector.tensor_reduce(stat[:, 1, t], xsq, X, ALU.add))
                nc.vector.tensor_scalar(stat[:, 1, t], stat[:, 1, t], 1.0 / E, EPS, ALU.mult, ALU.add)\
                  .then_inc(var_ready, 1)
                dve.wait_ge(sd_ready, b + 1)
                link(nc.vector.reciprocal(stat[:, 3, t], stat[:, 2, t]))
                link(nc.vector.tensor_tensor(stat[:, 4, t], stat[:, 3, t], stat[:, 3, t], ALU.mult))
                link(nc.vector.tensor_tensor(stat[:, 5, t], stat[:, 4, t], stat[:, 1, t], ALU.mult))
                link(nc.vector.tensor_scalar(stat[:, 6, t], stat[:, 5, t], -0.5, 1.5, ALU.mult, ALU.add))
                link(nc.vector.tensor_tensor(stat[:, 7, t], stat[:, 6, t], stat[:, 3, t], ALU.mult))
                nc.vector.tensor_tensor(xcb, xcb, stat[:, 7, t].unsqueeze(2).to_broadcast([P, QB, E]), ALU.mult)\
                  .then_inc(xn_ready, 1)
            for b in range(B):
                for i in range(2):
                    dve.wait_ge(high_ready, 2 * b + i + 1)
                    if b:
                        dve.wait_ge(low_ready, i + 1)
                    nc.vector.scalar_tensor_tensor(
                        out=rest[:, i, :], in0=ps[:, 2 + 2 * i:4 + 2 * i, :].rearrange("p a c -> p (a c)"),
                        scalar=b_qk[:, i:i + 1], in1=parts[:, i, 0, :], op0=ALU.add, op1=ALU.subtract)\
                      .then_inc(rest_ready, 1)
                dve.wait_ge(v_done, b + 1)
                for g in range(H // G):
                    nc.vector.tensor_tensor(
                        v_all[:, b * (H // G) + g, :, :, 0:D],
                        ps[:, 6:8, :].rearrange("p a (t h d) -> p (a t) h d", t=4, d=D)[:, :, g * G:(g + 1) * G, :],
                        b_v[:, g * G * D:(g + 1) * G * D].rearrange("p (h d) -> p h d", d=D).unsqueeze(1)
                        .to_broadcast([P, QB, G, D]), ALU.add).then_inc(v_ready, 1)

            def wide(a):
                return a.unsqueeze(2).to_broadcast([P, TILES, EXPERTS])

            rank_w = rank[:, :].unsqueeze(1).to_broadcast([P, TILES, EXPERTS])
            dve.wait_ge(consts_ready, 1)
            dve.wait_ge(logits_done, 1)
            lg = ps[:, 0, 0:TILES * EXPERTS].rearrange("p (t e) -> p t e", e=EXPERTS)
            link(nc.vector.tensor_reduce(rs[:, 0, :], lg, X, ALU.max))
            nc.vector.tensor_tensor(rt[:, 0, :, :], lg, wide(rs[:, 0, :]), ALU.subtract).then_inc(logits_cut, 1)
            dve.wait_ge(router_exp, 1)
            p = rt[:, 1, :, :]
            link(nc.vector.tensor_reduce(rs[:, 1, :], p, X, ALU.max))

            def first_of(v, top, eq, key, at, mask):
                link(nc.vector.tensor_tensor(rt[:, eq, :, :], v, wide(rs[:, top, :]), ALU.is_equal))
                link(nc.vector.tensor_tensor(rt[:, key, :, :], rt[:, eq, :, :], rank_w, ALU.mult))
                link(nc.vector.tensor_reduce(rs[:, at, :], rt[:, key, :, :], X, ALU.max))
                link(nc.vector.tensor_tensor(rt[:, mask, :, :], rt[:, key, :, :], wide(rs[:, at, :]), ALU.is_equal))

            first_of(p, 1, 2, 3, 2, 4)
            link(nc.vector.scalar_tensor_tensor(out=rt[:, 5, :, :], in0=rt[:, 4, :, :], scalar=-2.0, in1=p,
                                                op0=ALU.mult, op1=ALU.add))
            link(nc.vector.tensor_reduce(rs[:, 3, :], rt[:, 5, :, :], X, ALU.max))
            first_of(rt[:, 5, :, :], 3, 6, 7, 4, 8)
            link(nc.vector.tensor_tensor(rs[:, 5, :], rs[:, 1, :], rs[:, 3, :], ALU.add))
            link(nc.vector.reciprocal(rs[:, 6, :], rs[:, 5, :]))
            link(nc.vector.tensor_tensor(rt[:, 9, :, :], rt[:, 4, :, :], rt[:, 8, :, :], ALU.add))
            link(nc.vector.tensor_tensor(rt[:, 10, :, :], rt[:, 9, :, :], p, ALU.mult))
            nc.vector.tensor_tensor(rt[:, 11, :, :].rearrange("p t e -> p (t e)").rearrange("p (e t) -> p t e", t=TILES),
                                    rt[:, 10, :, :], wide(rs[:, 6, :]), ALU.mult).then_inc(combine_ready, 1)

            def ctx_norm(n, qc):
                at = n * CHUNKS + qc
                dve.wait_ge(raw_turned, at + 1)
                raw = ps[:, 7, :].rearrange("p (t g s) -> p t g s", t=4, s=SLOT)
                nc.vector.reciprocal(rsum[:, :, :], raw[:, :, :, D]).then_inc(ctx_step, 1)
                dve.wait_ge(ctx_step, at * CTX_STEPS + 1)
                nc.vector.tensor_tensor(
                    ctx_f[:, bass.ts(n, QB * G * D)].rearrange("p (t g d) -> p t g d", g=G, d=D)[:, 4 * qc:4 * qc + 4],
                    raw[:, :, :, 0:D], rsum[:, :, :].unsqueeze(3).to_broadcast([P, 4, G, D]), ALU.mult)\
                  .then_inc(ctx_step, 1)

            ctx_f = ctx_n[:, :, :, :].rearrange("p u t e -> p (u t e)")

            def raw_copy(n, qc):
                dve.wait_ge(pv_done, n * NB + LAST_STEP[qc] + 1)
                nc.vector.tensor_copy(raw_t[:, :], ps[:, 6, :]).then_inc(raw_copied, 1)

            def reduce_tile(n, i):
                qb, kc, pr = A_TILES[i]
                w, _ = span_a(i)
                k = 2 * (i % 2)
                dve.wait_ge(a_scored, n * NA + i + 1)
                nc.vector.tensor_reduce(mx[:, kc, :, pr, qb], ps[:, k:k + 2, 0:w], X, ALU.max).then_inc(a_reduced, 1)

            def hidden(n, s):
                dve.wait_ge(relu_done, n * NC + s + 1)
                nc.vector.tensor_tensor(hid[:, s % 2, :], gate[:, s % 2, :], ps[:, 4 + s % 2, TOK:2 * TOK], ALU.mult)\
                  .then_inc(hid_ready, 1)

            def split_max(n):
                dve.wait_ge(a_reduced, (n + 1) * NA)
                at = n * M_STEPS
                nc.vector.tensor_tensor(neg_m[:, :, :, :], mx[:, 0], mx[:, 1], ALU.max).then_inc(m_step, 1)
                dve.wait_ge(m_step, at + 1)
                nc.vector.tensor_scalar(m_parts[:, :, 0], neg_m[:, :, :, :], -1.0, None, ALU.mult).then_inc(m_step, 1)
                dve.wait_ge(m_step, at + 2)
                nc.vector.scalar_tensor_tensor(out=m_rest[:, 0], in0=neg_m[:, :, :, :], scalar=-1.0,
                                               in1=m_parts[:, :, 0], op0=ALU.mult, op1=ALU.subtract)\
                  .then_inc(m_step, 1)
                dve.wait_ge(m_step, at + 3)
                nc.vector.tensor_copy(m_parts[:, :, 1], m_rest[:, 0]).then_inc(m_step, 1)
                dve.wait_ge(m_step, at + 4)
                nc.vector.tensor_tensor(m_parts[:, :, 2], m_rest[:, 0], m_parts[:, :, 1], ALU.subtract)\
                  .then_inc(m_step, 1)

            def silu(n):
                dve.wait_ge(ez_done, n + 1)
                at = n * SILU_STEPS
                nc.vector.tensor_scalar(silu_b[:, 1, :], silu_b[:, 0, :], 1.0, None, ALU.add).then_inc(silu_step, 1)
                dve.wait_ge(silu_step, at + 1)
                nc.vector.reciprocal(silu_b[:, 2, :], silu_b[:, 1, :]).then_inc(silu_step, 1)
                dve.wait_ge(silu_step, at + 2)
                nc.vector.tensor_tensor(g_t[:, bass.ts(n, TOK)], ps[:, 7, 0:TOK], silu_b[:, 2, :], ALU.mult)\
                  .then_inc(silu_step, 1)

            def phase_a(n, before):
                for s in range(NC):
                    if s < A_SLOTS:
                        for i in range(A_PER):
                            reduce_tile(n, s * A_PER + i)
                            if i == 0:
                                hidden(n, s)
                    else:
                        hidden(n, s)
                    if s == 0 and before is not None:
                        ctx_norm(before, CHUNKS - 1)
                    if s == A_SLOTS - 1:
                        split_max(n)
                silu(n)

            def phase_b(n):
                for qc in range(CHUNKS):
                    raw_copy(n, qc)
                    if qc < CHUNKS - 1:
                        ctx_norm(n, qc)

            phase_a(0, None)
            with dve.Fori(1, UNITS) as n:
                phase_b(n - 1)
                phase_a(n, n - 1)
            phase_b(UNITS - 1)
            ctx_norm(UNITS - 1, CHUNKS - 1)
            for c in range(B * CHUNKS):
                k = 4 * (c % 2)
                dve.wait_ge(proj_done, c + 1)
                if c >= 2:
                    dve.wait_ge(y_turned, c - 1)
                nc.vector.scalar_tensor_tensor(out=y_t[:, c % 2, :], in0=ps[:, k + 1, :], scalar=b_o[:, 0:1],
                                               in1=g_t[:, c * CH:(c + 1) * CH], op0=ALU.add, op1=ALU.mult)\
                  .then_inc(y_ready, 1)
                dve.wait_ge(y_turned, c + 1)
                if c >= 2:
                    dve.wait_ge(stored[c % 2], 16 * (c // 2))
                nc.vector.tensor_tensor(o_sb[:, c % 2, :], ps[:, k + 2, :],
                                        x_sb[:, 4 * c:4 * c + 4, :].rearrange("p t e -> p (t e)"), ALU.add)\
                  .then_inc(o_ready, 1)

        @block.tensor
        def _(pe):
            sq = probs[:, :, :, :].rearrange("p a g c -> p (a g c)")
            pe.wait_ge(pool_step, EXPERTS + 1)
            for b in range(B):
                pe.wait_ge(xn_ready, b + 1)
                if b:
                    pe.wait_ge(xnt_ready, b)
                for t in range(QB):
                    mm = nc.tensor.transpose(ps[:, t // 4, (t % 4) * P:(t % 4 + 1) * P],
                                             sq[:, b * 1024 + t * E:b * 1024 + (t + 1) * E], ident[:, :])
                mm.then_inc(xn_turned, 1)
                pe.wait_ge(xnt_ready, b + 1)
                if b == 0:
                    pe.wait_ge(proj_loaded, 64)
                for i in range(2):
                    if b:
                        pe.wait_ge(rest_ready, 2 * b - 1 + i)
                    for c in range(CHUNKS):
                        mm = nc.tensor.matmul(ps[:, 2 + 2 * i + c, :], w_in_sb[:, i * E:(i + 1) * E],
                                              xn_t[:, b * S + c * CH:b * S + (c + 1) * CH], start=True, stop=True)
                    mm.then_inc(qk_done, 1)
                if b:
                    pe.wait_ge(v_ready, b * H // G)
                for t in range(QB):
                    mm = nc.tensor.matmul(ps[:, 6 + t // 4, (t % 4) * P:(t % 4 + 1) * P],
                                          xn_t[:, b * S + t * P:b * S + (t + 1) * P], w_in_sb[:, 2 * E:3 * E],
                                          start=True, stop=True)
                mm.then_inc(v_done, 1)
            for t in range(TILES):
                mm = nc.tensor.matmul(ps[:, 0, t * EXPERTS:(t + 1) * EXPERTS], xn_t[:, t * P:(t + 1) * P],
                                      wr_sb[:, :], start=True, stop=True)
            mm.then_inc(logits_done, 1)
            pe.wait_ge(combine_ready, 1)
            nc.tensor.transpose(ps[:, 1, 0:P], rt[:, 11, :, :].rearrange("p t e -> p (t e)"), ident[:, :])\
              .then_inc(combine_turned, 1)
            pe.wait_ge(rest_ready, 2 * B)
            pe.wait_ge(v_ready, B * H // G)
            pe.wait_ge(ffn_loaded, 80)
            pe.wait_ge(combine_copied, 1)

            def gate_up(n, s):
                e, c = s // FC, s % FC
                if c == 0:
                    pe.wait_ge(xcur_ready, n * (EXPERTS + 1) + e + 2)
                f = slice(c * P, (c + 1) * P)
                nc.tensor.matmul(ps[:, 4 + s % 2, 0:TOK], wg_sb[:, e, f], x_cur[:, :], start=True, stop=True)
                nc.tensor.matmul(ps[:, 4 + s % 2, TOK:2 * TOK], wu_sb[:, e, f], x_ce[:, e, :], start=True, stop=True)\
                  .then_inc(gu_done, 1)

            def down(n, s):
                pe.wait_ge(hid_ready, n * NC + s + 1)
                mm = nc.tensor.matmul(ps[:, 7, 0:TOK], wd_sb[:, s, :], hid[:, s % 2, :],
                                      start=(s == 0), stop=(s == NC - 1))
                if s == NC - 1:
                    mm.then_inc(ffn_done, 1)

            def score_a(n, i):
                qb, kc, pr = A_TILES[i]
                w, diagonal = span_a(i)
                if i >= 2:
                    pe.wait_ge(a_reduced, n * NA + i - 1)
                for hh in range(2):
                    bank = 2 * (i % 2) + hh
                    mm = nc.tensor.matmul(ps[:, bank, 0:w], q_a[:, pr, qb * P:(qb + 1) * P],
                                          k_a[:, pr, hh, kc * CH:kc * CH + w], start=True, stop=not diagonal)
                    if diagonal:
                        mm = nc.tensor.matmul(ps[:, bank, w - P:w], ident_h[:, :], mask_q[:, :],
                                              start=False, stop=True)
                mm.then_inc(a_scored, 1)

            def turn_raw(n, qc):
                pe.wait_ge(raw_copied, n * CHUNKS + qc + 1)
                for t in range(4):
                    mm = nc.tensor.transpose(ps[:, 7, t * P:(t + 1) * P], raw_t[:, t * P:(t + 1) * P], ident[:, :])
                mm.then_inc(raw_turned, 1)

            def phase_a(n, before):
                pe.wait_ge(a_loaded, n * 64 + 64)
                for s in range(NC):
                    if s < A_SLOTS:
                        score_a(n, s * A_PER)
                    gate_up(n, s)
                    if s < A_SLOTS:
                        for i in range(1, A_PER):
                            score_a(n, s * A_PER + i)
                    if s == 0 and before is not None:
                        turn_raw(before, CHUNKS - 1)
                    if s == 1 and before is not None:
                        pe.wait_ge(ctx_step, (before + 1) * CHUNKS * CTX_STEPS)
                    if s >= 1:
                        down(n, s - 1)
                    if s == A_SLOTS:
                        pe.wait_ge(m_step, (n + 1) * M_STEPS)
                        nc.tensor.transpose(ps[0:M_COLS, 6, 0:P // 2].bitcast(BF16),
                                            m_parts[:, :, :, :, :].rearrange("p c r a q -> p (c r a q)"),
                                            ident_h[:, :]).then_inc(m_turned, 1)
                down(n, NC - 1)

            def score_b(n, s, pr):
                i = s * PAIRS + pr
                _, kb = B_STEPS[s]
                q0, w, diagonal = span_b(s)
                if i >= 3:
                    pe.wait_ge(exp_done, n * NB * PAIRS + i - 2)
                for hh in range(2):
                    bank = 2 * (i % 3) + hh
                    mm = nc.tensor.matmul(ps[:, bank, 0:w], k_b[:, pr, hh, kb * P:(kb + 1) * P],
                                          q_b[:, pr, q0:q0 + w], start=True, stop=not diagonal)
                    if diagonal:
                        mm = nc.tensor.matmul(ps[:, bank, 0:P], ident_h[:, :], mask_k[:, :], start=False, stop=True)
                mm.then_inc(b_scored, 1)

            def weigh(n, s):
                qc, kb = B_STEPS[s]
                q0, w, _ = span_b(s)
                pe.wait_ge(exp_done, n * NB * PAIRS + (s + 1) * PAIRS)
                if kb == 0 and qc:
                    pe.wait_ge(raw_copied, n * CHUNKS + qc)
                for g in range(G):
                    mm = nc.tensor.matmul(ps[SLOT * g:SLOT * (g + 1), 6, CH - w:CH], v_b[:, kb, g, :],
                                          probs[:, s % 2, g, 0:w], start=(kb == 0), stop=(s == LAST_STEP[qc]))
                mm.then_inc(pv_done, 1)

            def phase_b(n):
                pe.wait_ge(ones_placed, 32)
                pe.wait_ge(b_loaded, n * 80 + 80)
                pe.wait_ge(m_loaded, n * 32 + 32)
                for s in range(NB):
                    for pr in range(PAIRS):
                        score_b(n, s, pr)
                    if s >= 1:
                        weigh(n, s - 1)
                    if s == LAST_STEP[0] + 3:
                        pe.wait_ge(silu_step, (n + 1) * SILU_STEPS)
                        turn_raw(n, 0)
                weigh(n, NB - 1)

            phase_a(0, None)
            with pe.Fori(1, UNITS) as n:
                phase_b(n - 1)
                phase_a(n, n - 1)
            phase_b(UNITS - 1)
            turn_raw(UNITS - 1, CHUNKS - 1)
            pe.wait_ge(ctx_step, UNITS * CHUNKS * CTX_STEPS)
            for c in range(B * CHUNKS):
                k = 4 * (c % 2)
                pe.wait_ge(ctx_gathered, c + 1)
                if c >= 2:
                    pe.wait_ge(ctxt_ready, c - 1)
                for t in range(4):
                    mm = nc.tensor.transpose(ps[:, k, t * P:(t + 1) * P], ctx_row[:, 4 * c + t, :], ident[:, :])
                mm.then_inc(ctx_turned, 1)
                pe.wait_ge(ctxt_ready, c + 1)
                if c >= 2:
                    pe.wait_ge(y_ready, c - 1)
                nc.tensor.matmul(ps[:, k + 1, :], w_out_sb[:, :], ctx_t[:, c % 2, :], start=True, stop=True)\
                  .then_inc(proj_done, 1)
                pe.wait_ge(y_ready, c + 1)
                if c >= 2:
                    pe.wait_ge(o_ready, c - 1)
                for t in range(4):
                    mm = nc.tensor.transpose(ps[:, k + 2, t * P:(t + 1) * P], y_t[:, c % 2, t * P:(t + 1) * P],
                                             ident[:, :])
                mm.then_inc(y_turned, 1)


def kernel(L0_attn_x, L0_attn_in_proj_w, L0_attn_in_proj_b, L0_attn_out_proj_w, L0_attn_out_proj_b,
           L0_ffn_Wr, L0_ffn_Wg, L0_ffn_Wu, L0_ffn_Wd):
    import numpy as np
    import concourse.bacc as bacc
    from concourse import mybir as mb
    from concourse.bass_utils import run_bass_kernel_spmd

    nc = bacc.Bacc("TRN2", target_bir_lowering=False, num_devices=1)
    b_in = np.ascontiguousarray(L0_attn_in_proj_b)
    arrays = {
        "x": np.ascontiguousarray(L0_attn_x),
        "w_in": np.ascontiguousarray(np.asarray(L0_attn_in_proj_w).T),
        "b_in": np.ascontiguousarray(b_in.reshape(3, -1).T),
        "b_in_row": b_in.reshape(1, -1),
        "w_out": np.ascontiguousarray(np.asarray(L0_attn_out_proj_w).T),
        "b_out": np.ascontiguousarray(L0_attn_out_proj_b).reshape(-1, 1),
        "w_router": np.ascontiguousarray(L0_ffn_Wr),
        "w_gate": np.ascontiguousarray(L0_ffn_Wg),
        "w_up": np.ascontiguousarray(L0_ffn_Wu),
        "w_down": np.ascontiguousarray(L0_ffn_Wd),
    }
    args = [nc.dram_tensor(n, a.shape, mb.dt.from_np(a.dtype), kind="ExternalInput").ap() for n, a in arrays.items()]
    out = nc.dram_tensor("out", (B, S, E), mb.dt.float32, kind="ExternalOutput").ap()
    build(nc, *args, out)
    r = run_bass_kernel_spmd(nc, [arrays], core_ids=[0])
    return r.results[0]["out"]
```

```python
from contextlib import ExitStack

import concourse.bass as bass
from concourse import mybir

F32 = mybir.dt.float32
F32R = mybir.dt.float32r
BF16 = mybir.dt.bfloat16
ALU = mybir.AluOpType
ACT = mybir.ActivationFunctionType
X = mybir.AxisListType.X

P = 128
B, S, E = 2, 1024, 128
H, D = 16, 8
G = 4
GROUPS = H // G
PAIRS = G // 2
UNITS = B * GROUPS
TILES = B * S // P
QB = S // P
CH = 512
CHUNKS = S // CH
EXPERTS, DFF = 8, 256
FC = DFF // P
TOK = B * S // UNITS
Q_PARTS = (0, 0, 0, 1, 1, 2)
K_PARTS = (0, 1, 2, 0, 1, 0)
NT = len(Q_PARTS)
ROWS = NT * D
HALF = P // 2
SLOT = P // G
VW = D + 1
SCALE = float(D) ** -0.5
EPS = 1e-5
MASKED = -1e30


def heads_of_tiles(w):
    return [(0, G)] if w * G <= 2 * CH else [(0, G // 2), (G // 2, G // 2)]


def span_a(qb, kc):
    return min(CH, (qb + 1) * P - kc * CH), kc == qb * P // CH


def span_b(qc, kb):
    q0 = max(qc * CH, kb * P)
    return q0, (qc + 1) * CH - q0, kb * P >= qc * CH


A_TILES = [(qb, kc, h0, nh) for qb in range(QB) for kc in range(qb * P // CH + 1)
           for h0, nh in heads_of_tiles(span_a(qb, kc)[0])]
B_STEPS = [(qc, kb) for qc in range(CHUNKS) for kb in range((qc + 1) * CH // P)]
B_TILES = [(s, h0, nh) for s, at in enumerate(B_STEPS) for h0, nh in heads_of_tiles(span_b(*at)[1])]
NA, NB, NBT = len(A_TILES), len(B_STEPS), len(B_TILES)
LAST_STEP = [max(i for i, (q, _) in enumerate(B_STEPS) if q == qc) for qc in range(CHUNKS)]
HOSTED = 10
TURN_STEP = LAST_STEP[0] + 3
NC = EXPERTS * FC
LAG = 3
RING = 4
MAX_SLOT = NA - HOSTED
XP = 4
M_STEPS, SILU_STEPS, CTX_STEPS = 5, 3, 2
M_COLS = 2 * 3 * PAIRS * QB
PE_ROUND = 12


def phase_1_order(first):
    tiles = list(range(0 if first else HOSTED, NA))
    order = []
    if first:
        order += [("max", i) for i in tiles[:PE_ROUND]]
        tiles = tiles[PE_ROUND:]
    for s in range(NC):
        order.append(("ffn", s))
        if tiles:
            order.append(("max", tiles.pop(0)))
            if not tiles:
                order.append(("maxima", 0))
    return order


def build(nc, x, w_in, b_in, b_in_row, w_out, b_out, w_router, w_gate, w_up, w_down, out):
    q_scr = nc.dram_tensor("q_scratch", (B, P, NT, S), BF16).ap()
    k_scr = nc.dram_tensor("k_scratch", (B, P, NT, S), BF16).ap()
    ce_scr = nc.dram_tensor("combine_scratch", (EXPERTS, B * S), F32).ap()

    ctx = ExitStack()
    with ctx:
        def sb(name, shape, dt=F32):
            return ctx.enter_context(nc.sbuf_tensor(name, shape, dt))

        def sem(name):
            return ctx.enter_context(nc.semaphore(name))

        ps = ctx.enter_context(nc.psum_tensor("ps", [P, 8, CH], F32))

        x_sb = sb("x_sb", [P, TILES, E])
        xn_t = sb("xn_t", [P, B * S])
        w_in_sb = sb("w_in_sb", [P, 3 * E])
        w_out_sb = sb("w_out_sb", [P, E])
        b_qk = sb("b_qk", [P, 2])
        b_v = sb("b_v", [P, E])
        b_o = sb("b_o", [P, 1])
        wr_sb = sb("wr_sb", [P, EXPERTS])
        w_hi = [sb(f"w_hi{i}", [P, EXPERTS * DFF], F32R) for i in range(3)]
        w_lo = [sb(f"w_lo{i}", [P, EXPERTS * DFF], F32R) for i in range(3)]
        ident = sb("ident", [P, P])
        ident_h = sb("ident_h", [P, P], BF16)
        mask_q = sb("mask_q", [P, P], BF16)
        mask_k = sb("mask_k", [P, P], BF16)
        rank = sb("rank", [P, EXPERTS])
        ones_rows = sb("ones_rows", [3, 2 * S], BF16)
        q_a = sb("q_a", [P, PAIRS, S], BF16)
        k_a = sb("k_a", [P, PAIRS, 2, S], BF16)
        q_b = sb("q_b", [P, PAIRS, S], BF16)
        k_b = sb("k_b", [P, PAIRS, 2, S], BF16)
        v_all = sb("v_all", [P, UNITS, QB, G, VW])
        v_b = sb("v_b", [P, QB, G, VW])
        ce_b = sb("ce_b", [P, EXPERTS, TOK])
        xw = sb("xw", [P, EXPERTS, TOK])
        xw_hi = sb("xw_hi", [P, EXPERTS, TOK], F32R)
        xw_lo = sb("xw_lo", [P, EXPERTS, TOK], F32R)
        xc_hi = sb("xc_hi", [P, TOK], F32R)
        xc_lo = sb("xc_lo", [P, TOK], F32R)
        early = sb("early", [P, 3 * S])
        hid_hi = sb("hid_hi", [P, RING, TOK], F32R)
        hid_lo = sb("hid_lo", [P, RING, TOK], F32R)
        probs = sb("probs", [P, 2, G, CH])
        mx = sb("mx", [P, CHUNKS, 2, PAIRS, QB])
        top_m = sb("top_m", [P, 2, PAIRS, QB])
        m_rest = sb("m_rest", [P, 2, PAIRS, QB])
        m_parts = sb("m_parts", [P, 2, 3, PAIRS, QB], BF16)
        m_t = sb("m_t", [M_COLS, P], BF16)
        rsum = sb("rsum", [P, 4, G])
        ctx_n = sb("ctx_n", [P, UNITS, QB, G * D])
        ctx_row = sb("ctx_row", [P, TILES, E])
        g_t = sb("g_t", [P, B * S])
        stat = sb("stat", [P, 8, TILES])
        rt = sb("rt", [P, 8, TILES, EXPERTS])
        rs = sb("rs", [P, 8, TILES])
        ce_t = sb("ce_t", [P, P])

        parts_0 = early[:, :].bitcast(BF16).rearrange("p (i r s) -> p i r s", i=2, r=3)
        hid = early[:, 0:RING * TOK].rearrange("p (r t) -> p r t", t=TOK)
        gate = early[:, 4 * TOK:6 * TOK].rearrange("p (r t) -> p r t", t=TOK)
        silu_b = early[:, 6 * TOK:9 * TOK].rearrange("p (r t) -> p r t", t=TOK)
        raw_t = early[:, 9 * TOK:9 * TOK + CH]
        x_cur = early[:, 9 * TOK + CH:10 * TOK + CH]
        w_raw = [ctx_n[:, :, :, :].rearrange("p u t e -> p (u t e)"), g_t[:, :],
                 ctx_row[:, :, :].rearrange("p t e -> p (t e)")]
        pool_of = probs[:, :, :, :].rearrange("p a g c -> p (a g c)")
        centre = [pool_of[:, b * S:(b + 1) * S] for b in range(B)]
        square = [pool_of[:, (2 + b) * S:(3 + b) * S] for b in range(B)]
        parts_1 = pool_of[:, S:4 * S].bitcast(BF16).rearrange("p (i r s) -> p i r s", i=2, r=3)
        parts = [parts_0, parts_1]
        rest = xw[:, :, :].rearrange("p (i e) t -> p i (e t)", i=2)
        xw_f = xw[:, :, :].rearrange("p e t -> p (e t)")
        ctx_t, y_t = xw_f[:, 0:CH], xw_f[:, CH:2 * CH]
        o_sb = [xw_f[:, (2 + i) * CH:(3 + i) * CH] for i in range(2)]
        ctx_f = w_raw[0]
        v_flat = v_all[:, :, :, :, :].rearrange("p u k g s -> p (u k g s)")

        x_loaded = [sem(f"x_loaded{b}") for b in range(B)]
        proj_loaded = sem("proj_loaded")
        router_loaded = sem("router_loaded")
        w_loaded = [sem(f"w_loaded{i}") for i in range(3)]
        out_loaded = sem("out_loaded")
        masks_ready = sem("masks_ready")
        ones_ready = sem("ones_ready")
        a_zeroed = sem("a_zeroed")
        b_zeroed = sem("b_zeroed")
        ones_placed = sem("ones_placed")
        pool_step = sem("pool_step")
        dve_step = sem("dve_step")
        centred = sem("centred")
        squared = sem("squared")
        var_ready = sem("var_ready")
        sd_ready = sem("sd_ready")
        xn_ready = sem("xn_ready")
        xn_turned = sem("xn_turned")
        xnt_ready = sem("xnt_ready")
        qk_done = sem("qk_done")
        v_done = sem("v_done")
        high_ready = sem("high_ready")
        rest_ready = sem("rest_ready")
        mid_ready = sem("mid_ready")
        low_ready = sem("low_ready")
        v_ready = sem("v_ready")
        w_hi_ready = sem("w_hi_ready")
        w_lo_ready = sem("w_lo_ready")
        scr_first = sem("scr_first")
        scr_others = sem("scr_others")
        scr_written = sem("scr_written")
        logits_done = sem("logits_done")
        logits_cut = sem("logits_cut")
        router_exp = sem("router_exp")
        combine_ready = sem("combine_ready")
        combine_turned = sem("combine_turned")
        combine_copied = sem("combine_copied")
        combine_written = sem("combine_written")
        a_loaded = sem("a_loaded")
        b_loaded = sem("b_loaded")
        m_loaded = sem("m_loaded")
        ce_loaded = sem("ce_loaded")
        weighted = sem("weighted")
        x_hi_ready = sem("x_hi_ready")
        x_lo_ready = sem("x_lo_ready")
        a_scored = sem("a_scored")
        a_reduced = sem("a_reduced")
        m_step = sem("m_step")
        m_turned = sem("m_turned")
        m_copied = sem("m_copied")
        gu_done = sem("gu_done")
        relu_done = sem("relu_done")
        hid_ready = sem("hid_ready")
        hid_hi_ready = sem("hid_hi_ready")
        hid_lo_ready = sem("hid_lo_ready")
        ffn_done = sem("ffn_done")
        ez_done = sem("ez_done")
        silu_step = sem("silu_step")
        b_scored = sem("b_scored")
        exp_done = sem("exp_done")
        pv_done = sem("pv_done")
        raw_copied = sem("raw_copied")
        raw_turned = sem("raw_turned")
        ctx_step = sem("ctx_step")
        ctx_gathered = sem("ctx_gathered")
        ctx_turned = sem("ctx_turned")
        ctxt_ready = sem("ctxt_ready")
        proj_done = sem("proj_done")
        y_ready = sem("y_ready")
        y_turned = sem("y_turned")
        o_ready = sem("o_ready")
        stored = [sem(f"stored{i}") for i in range(2)]

        block = ctx.enter_context(nc.Block())

        def gu_bank(s):
            return (2 if s in (12, 13) else 4) + s % 2

        def tile_view(bank, nh, w):
            if nh == G:
                return ps[:, bank:bank + 2, :].rearrange("p a c -> p (a c)")[:, 0:G * w]\
                    .rearrange("p (h w) -> p h w", w=w)
            return ps[:, bank:bank + 2, 0:w]

        @block.sync
        def _(sp):
            xv = x.rearrange("b (t p) e -> b p t e", p=P)

            def load_x(b):
                sp.dma_start(x_sb[:, b * QB:(b + 1) * QB, :], xv[b]).then_inc(x_loaded[b], 16)

            load_x(0)
            sp.dma_start(w_in_sb[:, :], w_in).then_inc(proj_loaded, 16)
            sp.dma_start(b_qk[:, :], b_in[:, 0:2]).then_inc(proj_loaded, 16)
            sp.dma_start(b_v[:, :], b_in_row[:, 2 * E:3 * E].to_broadcast([P, E])).then_inc(proj_loaded, 16)
            load_x(1)
            sp.dma_start(wr_sb[:, :], w_router).then_inc(router_loaded, 16)
            for i, w in enumerate((w_gate.rearrange("e d f -> d e f"), w_up.rearrange("e d f -> d e f"),
                                   w_down.rearrange("e (c f) d -> f (e c) d", f=P))):
                sp.dma_start(w_raw[i].rearrange("p (a b) -> p a b", b=w.shape[2]), w).then_inc(w_loaded[i], 16)
            sp.dma_start(w_out_sb[:, :], w_out).then_inc(out_loaded, 16)
            sp.dma_start(b_o[:, :], b_out).then_inc(out_loaded, 16)

            def store_parts(b, rows, done):
                n = rows.stop - rows.start
                for i, (scr, runs) in enumerate(((q_scr, ((0, 3, 0), (3, 2, 1), (5, 1, 2))),
                                                 (k_scr, ((0, 3, None), (3, 2, None), (5, 1, None))))):
                    for t, count, part in runs:
                        src = (parts[b][rows, i, 0:count, :] if part is None else
                               parts[b][rows, i, part:part + 1, :].to_broadcast([n, count, S]))
                        sp.dma_start(scr[b, rows, t:t + count, :], src).then_inc(done, 16)

            q_u = q_scr.rearrange("b (g a c d) t s -> (b g) c (d t) a s", g=GROUPS, a=PAIRS, c=2)
            k_u = k_scr.rearrange("b (g a c d) t s -> (b g) c (d t) a s", g=GROUPS, a=PAIRS, c=2)

            def load_qk(q_to, k_to, n, done):
                for hh in range(2):
                    r = slice(hh * HALF, hh * HALF + ROWS)
                    sp.dma_start(q_to[r, :, :], q_u[n, hh]).then_inc(done, 16)
                    sp.dma_start(k_to[r, :, hh, :], k_u[n, hh]).then_inc(done, 16)

            def load_ce(n):
                src = ce_scr[:, bass.ts(n, TOK)].unsqueeze(0).to_broadcast([P, EXPERTS, TOK])
                sp.dma_start(ce_b[:, :, :], src).then_inc(ce_loaded, 16)
                sp.dma_start(x_cur, xn_t[:, bass.ts(n, TOK)]).then_inc(ce_loaded, 16)

            def load_b(n):
                load_qk(q_b, k_b, n, b_loaded)
                sp.dma_start(v_b[:, :, :, :].rearrange("p k g s -> p (k g s)"),
                             v_flat[:, bass.ts(n, QB * G * VW)]).then_inc(b_loaded, 16)

            def load_m(n):
                sp.wait_ge(m_copied, n + 1)
                for hh in range(2):
                    r = hh * HALF + ROWS
                    sp.dma_start(q_b[r:r + 3, :, :].rearrange("r a (b q) -> r a b q", q=P),
                                 m_t[hh * M_COLS // 2:(hh + 1) * M_COLS // 2, :]).then_inc(m_loaded, 16)

            sp.wait_ge(ones_ready, 1)
            sp.wait_ge(b_zeroed, 1)
            for hh in range(2):
                r = hh * HALF + ROWS
                sp.dma_start(k_b[r:r + 3, :, hh, :], ones_rows[:, :].rearrange("r (a s) -> r a s", a=2))\
                  .then_inc(ones_placed, 16)
            sp.wait_ge(high_ready, 2)
            sp.wait_ge(mid_ready, 2)
            sp.wait_ge(low_ready, 2)
            store_parts(0, slice(0, G * D), scr_first)
            sp.wait_ge(scr_first, 16 * NT)
            sp.wait_ge(a_zeroed, 1)
            load_qk(q_a, k_a, 0, a_loaded)
            sp.wait_ge(v_ready, GROUPS)
            load_b(0)
            for g in range(1, GROUPS):
                store_parts(0, slice(g * G * D, (g + 1) * G * D), scr_others)
            sp.wait_ge(combine_copied, 1)
            sp.dma_start(ce_scr.rearrange("e (t k) -> (e t) k", k=P), ce_t[:, :]).then_inc(combine_written, 16)
            sp.wait_ge(combine_written, 16)
            sp.wait_ge(scr_others, 16 * NT * (GROUPS - 1))
            load_ce(0)
            sp.wait_ge(high_ready, 4)
            sp.wait_ge(mid_ready, 4)
            sp.wait_ge(low_ready, 4)
            store_parts(1, slice(0, P), scr_written)
            sp.wait_ge(v_ready, B * GROUPS)
            sp.wait_ge(scr_written, 16 * NT)
            load_m(0)
            sp.wait_ge(a_scored, NA)
            load_qk(q_a, k_a, 1, a_loaded)

            def unit_loads(n, following):
                sp.wait_ge(weighted, n * XP)
                load_ce(n)
                sp.wait_ge(pv_done, n * NB)
                load_b(n)
                load_m(n)
                if following:
                    sp.wait_ge(a_scored, n * NA + NA)
                    load_qk(q_a, k_a, n + 1, a_loaded)

            with sp.Fori(1, UNITS - 1) as n:
                unit_loads(n, True)
            unit_loads(UNITS - 1, False)
            ov = out.rearrange("b (t p) e -> p (b t) e", p=P)
            for c in range(B * CHUNKS):
                sp.wait_ge(o_ready, c + 1)
                sp.dma_start(ov[:, 4 * c:4 * c + 4, :], o_sb[c % 2].rearrange("p (t e) -> p t e", e=E))\
                  .then_inc(stored[c % 2], 16)
            for i in range(2):
                sp.wait_ge(stored[i], 16 * B * CHUNKS // 2)

        @block.gpsimd
        def _(pool):
            for m in (ident, ident_h, mask_q):
                nc.gpsimd.memset(m[:, :], 0.0)
            nc.gpsimd.memset(mask_k[:, :], 0.0).then_inc(pool_step, 1)
            pool.wait_ge(pool_step, 1)
            for m in (ident, ident_h):
                nc.gpsimd.affine_select(out=m[:, :], in_=m[:, :], compare_op=ALU.not_equal, fill=1.0, base=0,
                                        pattern=[[-1, P]], channel_multiplier=1)
            nc.gpsimd.affine_select(out=mask_q[:, :], in_=mask_q[:, :], compare_op=ALU.is_ge, fill=MASKED, base=0,
                                    pattern=[[-1, P]], channel_multiplier=1)
            nc.gpsimd.affine_select(out=mask_k[:, :], in_=mask_k[:, :], compare_op=ALU.is_ge, fill=MASKED,
                                    base=0, pattern=[[1, P]], channel_multiplier=-1).then_inc(masks_ready, 1)
            nc.gpsimd.memset(k_a[:, :, :, :].bitcast(F32), 0.0)
            nc.gpsimd.memset(q_a[:, :, :].bitcast(F32), 0.0).then_inc(a_zeroed, 1)
            nc.gpsimd.memset(ones_rows[:, :], 1.0).then_inc(ones_ready, 1)
            nc.gpsimd.memset(k_b[:, :, :, :].bitcast(F32), 0.0)
            nc.gpsimd.memset(q_b[:, :, :].bitcast(F32), 0.0).then_inc(b_zeroed, 1)

            def low_parts(b):
                for i in range(2):
                    pool.wait_ge(mid_ready, 2 * b + i + 1)
                    nc.gpsimd.tensor_tensor(parts[b][:, i, 2, :], rest[:, i, :], parts[b][:, i, 1, :],
                                            ALU.subtract).then_inc(low_ready, 1)

            low_parts(0)
            for i in range(3):
                pool.wait_ge(w_hi_ready, i + 1)
                nc.gpsimd.tensor_tensor(w_lo[i][:, :], w_raw[i], w_hi[i][:, :].bitcast(F32), ALU.subtract)\
                  .then_inc(w_lo_ready, 1)
            low_parts(1)

            def piece(i):
                return slice(i * EXPERTS // XP, (i + 1) * EXPERTS // XP)

            def inputs(n):
                def weigh_inputs(i):
                    nc.gpsimd.tensor_tensor(xw[:, piece(i), :], ce_b[:, piece(i), :],
                                            x_cur.unsqueeze(1).to_broadcast([P, EXPERTS // XP, TOK]), ALU.mult)\
                      .then_inc(weighted, 1)

                weigh_inputs(0)
                pool.wait_ge(x_hi_ready, n * (XP + 1) + 1)
                nc.gpsimd.tensor_tensor(xc_lo[:, :], x_cur, xc_hi[:, :].bitcast(F32), ALU.subtract)\
                  .then_inc(x_lo_ready, 1)
                for i in range(XP):
                    if i + 1 < XP:
                        weigh_inputs(i + 1)
                    pool.wait_ge(x_hi_ready, n * (XP + 1) + i + 2)
                    nc.gpsimd.tensor_tensor(xw_lo[:, piece(i), :], xw[:, piece(i), :],
                                            xw_hi[:, piece(i), :].bitcast(F32), ALU.subtract)\
                      .then_inc(x_lo_ready, 1)

            def hidden_low(n):
                for s in range(NC):
                    pool.wait_ge(hid_hi_ready, n * NC + s + 1)
                    nc.gpsimd.tensor_tensor(hid_lo[:, s % RING, :], hid[:, s % RING, :],
                                            hid_hi[:, s % RING, :].bitcast(F32), ALU.subtract)\
                      .then_inc(hid_lo_ready, 1)

            pool.wait_ge(low_ready, 2 * B)
            pool.wait_ge(ce_loaded, 32)
            inputs(0)
            hidden_low(0)
            with pool.Fori(1, UNITS) as n:
                pool.wait_ge(gu_done, n * NC)
                pool.wait_ge(ce_loaded, n * 32 + 32)
                inputs(n)
                hidden_low(n)

        @block.scalar
        def _(act):
            def two_banks(k):
                return ps[:, k:k + 2, :].rearrange("p a c -> p (a c)")

            def spread(b):
                act.wait_ge(centred, b + 1)
                nc.scalar.activation(square[b], centre[b], ACT.Square).then_inc(squared, 1)
                act.wait_ge(var_ready, b + 1)
                nc.scalar.activation(stat[:, 2, b * QB:(b + 1) * QB], stat[:, 1, b * QB:(b + 1) * QB], ACT.Sqrt)\
                  .then_inc(sd_ready, 1)

            def turned_x(b):
                act.wait_ge(xn_turned, b + 1)
                nc.scalar.activation(xn_t[:, b * S:(b + 1) * S], two_banks(0), ACT.Copy).then_inc(xnt_ready, 1)

            def high_parts(b):
                act.wait_ge(proj_loaded, 48)
                for i in range(2):
                    act.wait_ge(qk_done, 2 * b + i + 1)
                    nc.scalar.activation(parts[b][:, i, 0, :], two_banks(2 + 2 * i), ACT.Identity,
                                         bias=b_qk[:, i:i + 1]).then_inc(high_ready, 1)

            def mid_parts(b):
                for i in range(2):
                    act.wait_ge(rest_ready, 2 * b + i + 1)
                    nc.scalar.activation(parts[b][:, i, 1, :], rest[:, i, :], ACT.Copy).then_inc(mid_ready, 1)

            def weights_high(i):
                act.wait_ge(w_loaded[i], 16)
                nc.scalar.activation(w_hi[i][:, :], w_raw[i], ACT.Copy).then_inc(w_hi_ready, 1)

            spread(0)
            turned_x(0)
            high_parts(0)
            mid_parts(0)
            spread(1)
            weights_high(0)
            turned_x(1)
            high_parts(1)
            weights_high(1)
            weights_high(2)
            act.wait_ge(logits_cut, 1)
            nc.scalar.activation(rt[:, 1, :, :], rt[:, 0, :, :], ACT.Exp).then_inc(router_exp, 1)
            mid_parts(1)
            act.wait_ge(combine_turned, 1)
            nc.scalar.activation(ce_t[:, :], ps[:, 7, 0:P], ACT.Copy).then_inc(combine_copied, 1)

            def hidden_high(n, s):
                act.wait_ge(hid_ready, n * NC + s + 1)
                nc.scalar.activation(hid_hi[:, s % RING, :], hid[:, s % RING, :], ACT.Copy)\
                  .then_inc(hid_hi_ready, 1)

            def phase_1(n, first):
                order = phase_1_order(first)
                turn_at = order.index(("maxima", 0))
                for at, (what, s) in enumerate(order):
                    if what == "ffn":
                        act.wait_ge(gu_done, n * NC + s + 1)
                        nc.scalar.activation(gate[:, s % 2, :], ps[:, gu_bank(s), 0:TOK], ACT.Relu)\
                          .then_inc(relu_done, 1)
                        if s >= 1:
                            hidden_high(n, s - 1)
                    if at == turn_at + 2:
                        act.wait_ge(m_turned, n + 1)
                        nc.scalar.activation(m_t[:, :], ps[0:M_COLS, 6, 0:P // 2].bitcast(BF16), ACT.Copy)\
                          .then_inc(m_copied, 1)
                hidden_high(n, NC - 1)

            def phase_2(n):
                for i, (s, h0, nh) in enumerate(B_TILES):
                    w = span_b(*B_STEPS[s])[1]
                    act.wait_ge(b_scored, n * NBT + i + 1)
                    nc.scalar.activation(probs[:, s % 2, h0:h0 + nh, 0:w],
                                         tile_view(2 * (i % 2), nh, w), ACT.Exp, scale=SCALE).then_inc(exp_done, 1)
                    if i == 3:
                        act.wait_ge(ffn_done, n + 1)
                        nc.scalar.activation(silu_b[:, 0, :], ps[:, 7, 0:TOK], ACT.Exp, scale=-1.0)\
                          .then_inc(ez_done, 1)

            act.wait_ge(scr_others, 16 * NT * (GROUPS - 1))
            phase_1(0, True)
            act.wait_ge(scr_written, 16 * NT)
            with act.Fori(1, UNITS) as n:
                phase_2(n - 1)
                phase_1(n, False)
            phase_2(UNITS - 1)

        @block.vector
        def _(dve):
            steps = [0]

            def link(ins):
                steps[0] += 1
                ins.then_inc(dve_step, 1)
                dve.wait_ge(dve_step, steps[0])

            def layernorm(b):
                t = slice(b * QB, (b + 1) * QB)
                xc = centre[b].rearrange("p (t e) -> p t e", e=E)
                xsq = square[b].rearrange("p (t e) -> p t e", e=E)
                dve.wait_ge(x_loaded[b], 16)
                link(nc.vector.tensor_reduce(stat[:, 0, t], x_sb[:, t, :], X, ALU.add))
                link(nc.vector.tensor_scalar(stat[:, 0, t], stat[:, 0, t], 1.0 / E, None, ALU.mult))
                nc.vector.tensor_tensor(xc, x_sb[:, t, :], stat[:, 0, t].unsqueeze(2).to_broadcast([P, QB, E]),
                                        ALU.subtract).then_inc(centred, 1)
                dve.wait_ge(squared, b + 1)
                link(nc.vector.tensor_reduce(stat[:, 1, t], xsq, X, ALU.add))
                nc.vector.tensor_scalar(stat[:, 1, t], stat[:, 1, t], 1.0 / E, EPS, ALU.mult, ALU.add)\
                  .then_inc(var_ready, 1)
                dve.wait_ge(sd_ready, b + 1)
                link(nc.vector.reciprocal(stat[:, 3, t], stat[:, 2, t]))
                link(nc.vector.tensor_tensor(stat[:, 4, t], stat[:, 3, t], stat[:, 3, t], ALU.mult))
                link(nc.vector.tensor_tensor(stat[:, 5, t], stat[:, 4, t], stat[:, 1, t], ALU.mult))
                link(nc.vector.tensor_scalar(stat[:, 6, t], stat[:, 5, t], -0.5, 1.5, ALU.mult, ALU.add))
                link(nc.vector.tensor_tensor(stat[:, 7, t], stat[:, 6, t], stat[:, 3, t], ALU.mult))
                nc.vector.tensor_tensor(xc, xc, stat[:, 7, t].unsqueeze(2).to_broadcast([P, QB, E]), ALU.mult)\
                  .then_inc(xn_ready, 1)

            def rests(b):
                dve.wait_ge(proj_loaded, 48)
                for i in range(2):
                    dve.wait_ge(high_ready, 2 * b + i + 1)
                    if b:
                        dve.wait_ge(low_ready, i + 1)
                    nc.vector.scalar_tensor_tensor(
                        out=rest[:, i, :], in0=ps[:, 2 + 2 * i:4 + 2 * i, :].rearrange("p a c -> p (a c)"),
                        scalar=b_qk[:, i:i + 1], in1=parts[b][:, i, 0, :], op0=ALU.add, op1=ALU.subtract)\
                      .then_inc(rest_ready, 1)

            def values(b):
                dve.wait_ge(v_done, b + 1)
                bank = 4 if b else 6
                for g in range(GROUPS):
                    nc.vector.tensor_tensor(
                        v_all[:, b * GROUPS + g, :, :, 0:D],
                        ps[:, bank:bank + 2, :].rearrange("p a (t h d) -> p (a t) h d", t=4, d=D)
                        [:, :, g * G:(g + 1) * G, :],
                        b_v[:, g * G * D:(g + 1) * G * D].rearrange("p (h d) -> p h d", d=D).unsqueeze(1)
                        .to_broadcast([P, QB, G, D]), ALU.add).then_inc(v_ready, 1)

            def wide(a):
                return a.unsqueeze(2).to_broadcast([P, TILES, EXPERTS])

            def router():
                rank_w = rank[:, :].unsqueeze(1).to_broadcast([P, TILES, EXPERTS])
                dve.wait_ge(logits_done, 1)
                lg = ps[:, 6, 0:TILES * EXPERTS].rearrange("p (t e) -> p t e", e=EXPERTS)
                link(nc.vector.tensor_reduce(rs[:, 0, :], lg, X, ALU.max))
                nc.vector.tensor_tensor(rt[:, 0, :, :], lg, wide(rs[:, 0, :]), ALU.subtract).then_inc(logits_cut, 1)
                dve.wait_ge(router_exp, 1)
                p = rt[:, 1, :, :]
                link(nc.vector.tensor_reduce(rs[:, 1, :], p, X, ALU.max))

                def first_of(v, top, eq, key, at, mask):
                    link(nc.vector.tensor_tensor(rt[:, eq, :, :], v, wide(rs[:, top, :]), ALU.is_equal))
                    link(nc.vector.tensor_tensor(rt[:, key, :, :], rt[:, eq, :, :], rank_w, ALU.mult))
                    link(nc.vector.tensor_reduce(rs[:, at, :], rt[:, key, :, :], X, ALU.max))
                    link(nc.vector.tensor_tensor(rt[:, mask, :, :], rt[:, key, :, :], wide(rs[:, at, :]),
                                                 ALU.is_equal))

                first_of(p, 1, 2, 3, 2, 4)
                link(nc.vector.scalar_tensor_tensor(out=rt[:, 5, :, :], in0=rt[:, 4, :, :], scalar=-2.0, in1=p,
                                                    op0=ALU.mult, op1=ALU.add))
                link(nc.vector.tensor_reduce(rs[:, 3, :], rt[:, 5, :, :], X, ALU.max))
                first_of(rt[:, 5, :, :], 3, 2, 3, 4, 6)
                link(nc.vector.tensor_tensor(rs[:, 5, :], rs[:, 1, :], rs[:, 3, :], ALU.add))
                nc.vector.tensor_tensor(rt[:, 7, :, :], rt[:, 4, :, :], rt[:, 6, :, :], ALU.add)
                link(nc.vector.reciprocal(rs[:, 6, :], rs[:, 5, :]))
                link(nc.vector.tensor_tensor(rt[:, 2, :, :], rt[:, 7, :, :], p, ALU.mult))
                nc.vector.tensor_tensor(
                    rt[:, 3, :, :].rearrange("p t e -> p (t e)").rearrange("p (e t) -> p t e", t=TILES),
                    rt[:, 2, :, :], wide(rs[:, 6, :]), ALU.mult).then_inc(combine_ready, 1)

            for e in range(EXPERTS):
                nc.vector.memset(rank[:, e:e + 1], float(EXPERTS - e))
            nc.vector.memset(v_all[:, :, :, :, D:VW], 1.0)
            link(nc.vector.memset(mx[:, :, :, :, :], 4 * MASKED))
            layernorm(0)
            rests(0)
            values(0)
            layernorm(1)
            rests(1)
            values(1)
            router()

            def inputs_high(n, i):
                if i == 0:
                    dve.wait_ge(ce_loaded, n * 32 + 32)
                    nc.vector.tensor_copy(xc_hi[:, :], x_cur).then_inc(x_hi_ready, 1)
                else:
                    e = slice((i - 1) * EXPERTS // XP, i * EXPERTS // XP)
                    dve.wait_ge(weighted, n * XP + i)
                    nc.vector.tensor_copy(xw_hi[:, e, :], xw[:, e, :]).then_inc(x_hi_ready, 1)

            def raw_copy(n, qc):
                dve.wait_ge(pv_done, n * NB + LAST_STEP[qc] + 1)
                nc.vector.tensor_copy(raw_t, ps[:, 6, :]).then_inc(raw_copied, 1)

            def ctx_norm(n, qc):
                at = n * CHUNKS + qc
                dve.wait_ge(raw_turned, at + 1)
                raw = ps[:, 7, :].rearrange("p (t g s) -> p t g s", t=4, s=SLOT)
                nc.vector.reciprocal(rsum[:, :, :], raw[:, :, :, D]).then_inc(ctx_step, 1)
                dve.wait_ge(ctx_step, at * CTX_STEPS + 1)
                nc.vector.tensor_tensor(
                    ctx_f[:, bass.ts(n, QB * G * D)].rearrange("p (t g d) -> p t g d", g=G, d=D)[:, 4 * qc:4 * qc + 4],
                    raw[:, :, :, 0:D], rsum[:, :, :].unsqueeze(3).to_broadcast([P, 4, G, D]), ALU.mult)\
                  .then_inc(ctx_step, 1)

            def reduce_tile(n, i, bank):
                qb, kc, h0, nh = A_TILES[i]
                w, _ = span_a(qb, kc)
                dve.wait_ge(a_scored, n * NA + i + 1)
                src = tile_view(bank, nh, w).rearrange("p (a c) w -> p a c w", c=2)
                dst = mx[:, kc, :, h0 // 2:(h0 + nh) // 2, qb].rearrange("p c a -> p a c")
                nc.vector.tensor_reduce(dst, src, X, ALU.max).then_inc(a_reduced, 1)

            def hidden(n, s):
                dve.wait_ge(relu_done, n * NC + s + 1)
                nc.vector.tensor_tensor(hid[:, s % RING, :], gate[:, s % 2, :], ps[:, gu_bank(s), TOK:2 * TOK],
                                        ALU.mult).then_inc(hid_ready, 1)

            def split_max(n):
                dve.wait_ge(a_reduced, n * NA + NA)
                at = n * M_STEPS
                nc.vector.tensor_tensor(top_m[:, :, :, :], mx[:, 0], mx[:, 1], ALU.max).then_inc(m_step, 1)
                dve.wait_ge(m_step, at + 1)
                nc.vector.tensor_scalar(m_parts[:, :, 0], top_m[:, :, :, :], -1.0, None, ALU.mult).then_inc(m_step, 1)
                dve.wait_ge(m_step, at + 2)
                nc.vector.scalar_tensor_tensor(out=m_rest[:, :, :, :], in0=top_m[:, :, :, :], scalar=-1.0,
                                               in1=m_parts[:, :, 0], op0=ALU.mult, op1=ALU.subtract)\
                  .then_inc(m_step, 1)
                dve.wait_ge(m_step, at + 3)
                nc.vector.tensor_copy(m_parts[:, :, 1], m_rest[:, :, :, :]).then_inc(m_step, 1)
                dve.wait_ge(m_step, at + 4)
                nc.vector.tensor_tensor(m_parts[:, :, 2], m_rest[:, :, :, :], m_parts[:, :, 1], ALU.subtract)\
                  .then_inc(m_step, 1)

            def silu(n):
                dve.wait_ge(ez_done, n + 1)
                at = n * SILU_STEPS
                nc.vector.tensor_scalar(silu_b[:, 1, :], silu_b[:, 0, :], 1.0, None, ALU.add).then_inc(silu_step, 1)
                dve.wait_ge(silu_step, at + 1)
                nc.vector.reciprocal(silu_b[:, 2, :], silu_b[:, 1, :]).then_inc(silu_step, 1)
                dve.wait_ge(silu_step, at + 2)
                nc.vector.tensor_tensor(g_t[:, bass.ts(n, TOK)], ps[:, 7, 0:TOK], silu_b[:, 2, :], ALU.mult)\
                  .then_inc(silu_step, 1)

            def gather(c):
                b, t0 = c // CHUNKS, (c % CHUNKS) * 4
                dve.wait_ge(ctx_step, ((b * GROUPS + GROUPS - 1) * CHUNKS + c % CHUNKS + 1) * CTX_STEPS)
                nc.vector.tensor_copy(
                    ctx_row[:, 4 * c:4 * c + 4, :].rearrange("p t (g e) -> p t g e", g=GROUPS),
                    ctx_n[:, b * GROUPS:(b + 1) * GROUPS, t0:t0 + 4, :].rearrange("p g t e -> p t g e"))\
                  .then_inc(ctx_gathered, 1)

            def turned_ctx(c):
                dve.wait_ge(ctx_turned, c + 1)
                nc.vector.tensor_copy(ctx_t, ps[:, 4 + 3 * c % 2, :]).then_inc(ctxt_ready, 1)

            def gated(c):
                dve.wait_ge(proj_done, c + 1)
                if c == 0:
                    dve.wait_ge(out_loaded, 32)
                dve.wait_ge(silu_step, ((c + 1) * CH // TOK) * SILU_STEPS)
                nc.vector.scalar_tensor_tensor(out=y_t, in0=ps[:, 4 + (3 * c + 1) % 2, :], scalar=b_o[:, 0:1],
                                               in1=g_t[:, c * CH:(c + 1) * CH], op0=ALU.add, op1=ALU.mult)\
                  .then_inc(y_ready, 1)

            def residual(c):
                dve.wait_ge(y_turned, c + 1)
                if c >= 2:
                    dve.wait_ge(stored[c % 2], 16 * (c // 2))
                nc.vector.tensor_tensor(o_sb[c % 2], ps[:, 4 + 3 * c % 2, :],
                                        x_sb[:, 4 * c:4 * c + 4, :].rearrange("p t e -> p (t e)"), ALU.add)\
                  .then_inc(o_ready, 1)

            def phase_1(n, first):
                for at, (what, i) in enumerate(phase_1_order(first)):
                    if what == "max":
                        reduce_tile(n, i, 2 * (i % 2))
                    elif what == "ffn":
                        if first and i == 0:
                            for k in range(XP + 1):
                                inputs_high(n, k)
                        hidden(n, i)
                    else:
                        split_max(n)
                    if not first and at == 1:
                        ctx_norm(n - 1, CHUNKS - 1)

            def phase_2(n, following):
                for s in range(1, HOSTED + 1):
                    reduce_tile(following, s - 1, 4)
                    if s == 2:
                        silu(n)
                    if s == LAST_STEP[0]:
                        raw_copy(n, 0)
                    if s == TURN_STEP - 1:
                        ctx_norm(n, 0)
                    if s >= HOSTED - XP:
                        inputs_high(following, s - HOSTED + XP)
                raw_copy(n, CHUNKS - 1)

            phase_1(0, True)
            with dve.Fori(1, UNITS) as n:
                phase_2(n - 1, n)
                phase_1(n, False)
            gather(0)
            gather(1)
            turned_ctx(0)
            silu(UNITS - 1)
            gated(0)
            residual(0)
            turned_ctx(1)
            raw_copy(UNITS - 1, 0)
            gated(1)
            residual(1)
            ctx_norm(UNITS - 1, 0)
            gather(2)
            turned_ctx(2)
            gated(2)
            residual(2)
            raw_copy(UNITS - 1, 1)
            ctx_norm(UNITS - 1, 1)
            gather(3)
            turned_ctx(3)
            gated(3)
            residual(3)

        @block.tensor
        def _(pe):
            def turn_x(b):
                pe.wait_ge(xn_ready, b + 1)
                if b:
                    pe.wait_ge(xnt_ready, b)
                for t in range(QB):
                    mm = nc.tensor.transpose(ps[:, t // 4, (t % 4) * P:(t % 4 + 1) * P],
                                             centre[b][:, t * E:(t + 1) * E], ident[:, :])
                mm.then_inc(xn_turned, 1)

            def project_qk(b):
                pe.wait_ge(xnt_ready, b + 1)
                for i in range(2):
                    if b:
                        pe.wait_ge(rest_ready, i + 1)
                    for c in range(CHUNKS):
                        mm = nc.tensor.matmul(ps[:, 2 + 2 * i + c, :], w_in_sb[:, i * E:(i + 1) * E],
                                              xn_t[:, b * S + c * CH:b * S + (c + 1) * CH], start=True, stop=True)
                    mm.then_inc(qk_done, 1)

            def project_v(b, bank):
                for t in range(QB):
                    mm = nc.tensor.matmul(ps[:, bank + t // 4, (t % 4) * P:(t % 4 + 1) * P],
                                          xn_t[:, b * S + t * P:b * S + (t + 1) * P], w_in_sb[:, 2 * E:3 * E],
                                          start=True, stop=True)
                mm.then_inc(v_done, 1)

            pe.wait_ge(masks_ready, 1)
            turn_x(0)
            pe.wait_ge(proj_loaded, 48)
            project_qk(0)
            project_v(0, 6)
            turn_x(1)
            project_qk(1)
            pe.wait_ge(router_loaded, 16)
            pe.wait_ge(v_ready, GROUPS)
            for t in range(TILES):
                mm = nc.tensor.matmul(ps[:, 6, t * EXPERTS:(t + 1) * EXPERTS], xn_t[:, t * P:(t + 1) * P],
                                      wr_sb[:, :], start=True, stop=True)
            mm.then_inc(logits_done, 1)
            pe.wait_ge(rest_ready, 2 * B)
            project_v(1, 4)
            pe.wait_ge(combine_ready, 1)
            nc.tensor.transpose(ps[:, 7, 0:P], rt[:, 3, :, :].rearrange("p t e -> p (t e)"), ident[:, :])\
              .then_inc(combine_turned, 1)

            def three(out_ap, hi, lo, x_hi, x_lo, start=True, stop=True):
                nc.tensor.matmul(out_ap, hi, x_hi, start=start, stop=False)
                nc.tensor.matmul(out_ap, hi, x_lo, start=False, stop=False)
                return nc.tensor.matmul(out_ap, lo, x_hi, start=False, stop=stop)

            def gate_up(n, s):
                e, c = s // FC, s % FC
                if c == 0 and e % (EXPERTS // XP) == 0:
                    pe.wait_ge(x_lo_ready, n * (XP + 1) + e * XP // EXPERTS + 2)
                f = slice(e * DFF + c * P, e * DFF + (c + 1) * P)
                k = gu_bank(s)
                before = [t for t in range(s) if gu_bank(t) == k]
                if before:
                    pe.wait_ge(hid_ready, n * NC + before[-1] + 1)
                three(ps[:, k, 0:TOK], w_hi[0][:, f], w_lo[0][:, f], xc_hi[:, :], xc_lo[:, :])
                three(ps[:, k, TOK:2 * TOK], w_hi[1][:, f], w_lo[1][:, f], xw_hi[:, e, :], xw_lo[:, e, :])\
                    .then_inc(gu_done, 1)

            def down(n, s):
                pe.wait_ge(hid_lo_ready, n * NC + s + 1)
                f = slice(s * E, (s + 1) * E)
                mm = three(ps[:, 7, 0:TOK], w_hi[2][:, f], w_lo[2][:, f], hid_hi[:, s % RING, :],
                           hid_lo[:, s % RING, :], start=(s == 0), stop=(s == NC - 1))
                if s == NC - 1:
                    mm.then_inc(ffn_done, 1)

            def score(bank, h0, nh, w, stationary, moving, mask_at, mask):
                view = tile_view(bank, nh, w)
                for h in range(nh):
                    mm = nc.tensor.matmul(view[:, h, :], stationary(h0 + h), moving(h0 + h),
                                          start=True, stop=mask_at is None)
                    if mask_at is not None:
                        mm = nc.tensor.matmul(view[:, h, mask_at:mask_at + P], ident_h[:, :], mask[:, :],
                                              start=False, stop=True)
                return mm

            def score_a(n, i, bank):
                qb, kc, h0, nh = A_TILES[i]
                w, diagonal = span_a(qb, kc)
                score(bank, h0, nh, w, lambda h: q_a[:, h // 2, qb * P:(qb + 1) * P],
                      lambda h: k_a[:, h // 2, h % 2, kc * CH:kc * CH + w],
                      w - P if diagonal else None, mask_q).then_inc(a_scored, 1)

            def score_b(n, i):
                s, h0, nh = B_TILES[i]
                q0, w, diagonal = span_b(*B_STEPS[s])
                kb = B_STEPS[s][1]
                if i >= 2:
                    pe.wait_ge(exp_done, n * NBT + i - 1)
                score(2 * (i % 2), h0, nh, w, lambda h: k_b[:, h // 2, h % 2, kb * P:(kb + 1) * P],
                      lambda h: q_b[:, h // 2, q0:q0 + w], 0 if diagonal else None, mask_k).then_inc(b_scored, 1)

            def weigh(n, s):
                qc, kb = B_STEPS[s]
                w = span_b(qc, kb)[1]
                tiles = max(i for i, t in enumerate(B_TILES) if t[0] == s) + 1
                pe.wait_ge(exp_done, n * NBT + tiles)
                if kb == 0 and qc:
                    pe.wait_ge(raw_copied, n * CHUNKS + qc)
                for g in range(G):
                    mm = nc.tensor.matmul(ps[SLOT * g:SLOT * g + VW, 6, CH - w:CH], v_b[:, kb, g, :],
                                          probs[:, s % 2, g, 0:w], start=(kb == 0), stop=(s == LAST_STEP[qc]))
                mm.then_inc(pv_done, 1)

            def turn_raw(n, qc):
                pe.wait_ge(raw_copied, n * CHUNKS + qc + 1)
                for t in range(4):
                    mm = nc.tensor.transpose(ps[:, 7, t * P:(t + 1) * P], raw_t[:, t * P:(t + 1) * P], ident[:, :])
                mm.then_inc(raw_turned, 1)

            def turn_max(n):
                pe.wait_ge(m_step, n * M_STEPS + M_STEPS)
                nc.tensor.transpose(ps[0:M_COLS, 6, 0:P // 2].bitcast(BF16),
                                    m_parts[:, :, :, :, :].rearrange("p c r a q -> p (c r a q)"),
                                    ident_h[:, :]).then_inc(m_turned, 1)

            def phase_1(n, first):
                order = phase_1_order(first)
                turn_at = order.index(("maxima", 0)) + 1
                for at, (what, i) in enumerate(order):
                    if what == "max":
                        if i >= (0 if first else HOSTED) + 2:
                            pe.wait_ge(a_reduced, n * NA + i - 1)
                        score_a(n, i, 2 * (i % 2))
                    elif what == "ffn":
                        if not first and i == 0:
                            pe.wait_ge(a_reduced, n * NA + HOSTED)
                        if i == 12:
                            pe.wait_ge(a_reduced, n * NA + NA)
                        gate_up(n, i)
                        if not first and i == 1:
                            turn_raw(n - 1, CHUNKS - 1)
                        if not first and i == LAG:
                            pe.wait_ge(ctx_step, n * CHUNKS * CTX_STEPS)
                        if i >= LAG:
                            down(n, i - LAG)
                    if at == turn_at:
                        turn_max(n)

            def phase_2(n, beside):
                pe.wait_ge(b_loaded, n * 80 + 80)
                pe.wait_ge(m_loaded, n * 32 + 32)
                tile = 0
                for s in range(NB):
                    while tile < NBT and B_TILES[tile][0] == s:
                        score_b(n, tile)
                        if s == 0:
                            down(n, NC - LAG + tile)
                        tile += 1
                    if s == 0:
                        down(n, NC - 1)
                    if s >= 1:
                        weigh(n, s - 1)
                    if s == TURN_STEP:
                        pe.wait_ge(silu_step, n * SILU_STEPS + SILU_STEPS)
                        turn_raw(n, 0)
                    beside(s)
                weigh(n, NB - 1)

            def hosted(following):
                def beside(s):
                    if s == 1:
                        pe.wait_ge(a_loaded, following * 64 + 64)
                    if 1 <= s <= HOSTED:
                        if s >= 2:
                            pe.wait_ge(a_reduced, following * NA + s - 1)
                        score_a(following, s - 1, 4)
                return beside

            def turn_ctx(c):
                pe.wait_ge(ctx_gathered, c + 1)
                for t in range(4):
                    mm = nc.tensor.transpose(ps[:, 4 + 3 * c % 2, t * P:(t + 1) * P], ctx_row[:, 4 * c + t, :],
                                             ident[:, :])
                mm.then_inc(ctx_turned, 1)

            def project(c):
                pe.wait_ge(ctxt_ready, c + 1)
                if c == 0:
                    pe.wait_ge(out_loaded, 32)
                else:
                    pe.wait_ge(o_ready, c)
                nc.tensor.matmul(ps[:, 4 + (3 * c + 1) % 2, :], w_out_sb[:, :], ctx_t, start=True, stop=True)\
                  .then_inc(proj_done, 1)

            def turn_y(c):
                pe.wait_ge(y_ready, c + 1)
                for t in range(4):
                    mm = nc.tensor.transpose(ps[:, 4 + 3 * c % 2, t * P:(t + 1) * P], y_t[:, t * P:(t + 1) * P],
                                             ident[:, :])
                mm.then_inc(y_turned, 1)

            pe.wait_ge(a_loaded, 64)
            pe.wait_ge(w_lo_ready, 3)
            pe.wait_ge(ones_placed, 32)
            phase_1(0, True)
            with pe.Fori(1, UNITS) as n:
                phase_2(n - 1, hosted(n))
                phase_1(n, False)
            output = {1: (turn_ctx, 0), 2: (project, 0), 3: (turn_y, 0), 4: (turn_ctx, 1), 5: (project, 1),
                      7: (turn_y, 1), 9: (turn_ctx, 2), 10: (project, 2), 11: (turn_y, 2)}

            def output_beside(s):
                if s in output:
                    step, c = output[s]
                    step(c)

            phase_2(UNITS - 1, output_beside)
            turn_raw(UNITS - 1, CHUNKS - 1)
            turn_ctx(3)
            project(3)
            turn_y(3)


def kernel(L0_attn_x, L0_attn_in_proj_w, L0_attn_in_proj_b, L0_attn_out_proj_w, L0_attn_out_proj_b,
           L0_ffn_Wr, L0_ffn_Wg, L0_ffn_Wu, L0_ffn_Wd):
    import numpy as np
    import concourse.bacc as bacc
    from concourse import mybir as mb
    from concourse.bass_utils import run_bass_kernel_spmd

    nc = bacc.Bacc("TRN2", target_bir_lowering=False, num_devices=1)
    b_in = np.ascontiguousarray(L0_attn_in_proj_b)
    arrays = {
        "x": np.ascontiguousarray(L0_attn_x),
        "w_in": np.ascontiguousarray(np.asarray(L0_attn_in_proj_w).T),
        "b_in": np.ascontiguousarray(b_in.reshape(3, -1).T),
        "b_in_row": b_in.reshape(1, -1),
        "w_out": np.ascontiguousarray(np.asarray(L0_attn_out_proj_w).T),
        "b_out": np.ascontiguousarray(L0_attn_out_proj_b).reshape(-1, 1),
        "w_router": np.ascontiguousarray(L0_ffn_Wr),
        "w_gate": np.ascontiguousarray(L0_ffn_Wg),
        "w_up": np.ascontiguousarray(L0_ffn_Wu),
        "w_down": np.ascontiguousarray(L0_ffn_Wd),
    }
    args = [nc.dram_tensor(n, a.shape, mb.dt.from_np(a.dtype), kind="ExternalInput").ap() for n, a in arrays.items()]
    out = nc.dram_tensor("out", (B, S, E), mb.dt.float32, kind="ExternalOutput").ap()
    build(nc, *args, out)
    r = run_bass_kernel_spmd(nc, [arrays], core_ids=[0])
    return r.results[0]["out"]
```

```python
from contextlib import ExitStack

import concourse.bass as bass
from concourse import mybir

F32 = mybir.dt.float32
F32R = mybir.dt.float32r
BF16 = mybir.dt.bfloat16
ALU = mybir.AluOpType
ACT = mybir.ActivationFunctionType
X = mybir.AxisListType.X

P = 128
B, S, E = 2, 1024, 128
H, D = 16, 8
G = 4
GROUPS = H // G
PAIRS = G // 2
UNITS = B * GROUPS
TILES = B * S // P
QB = S // P
CH = 512
CHUNKS = S // CH
EXPERTS, DFF = 8, 256
FC = DFF // P
TOK = B * S // UNITS
Q_PARTS = (0, 0, 0, 1, 1, 2)
K_PARTS = (0, 1, 2, 0, 1, 0)
NT = len(Q_PARTS)
ROWS = NT * D
HALF = P // 2
SLOT = P // G
VW = D + 1
SCALE = float(D) ** -0.5
EPS = 1e-5
MASKED = -1e30


OTHERS = (GROUPS - 1) * G * D


def heads_of_tiles(w):
    return [(0, G)] if w * G <= 2 * CH else [(0, G // 2), (G // 2, G // 2)]


def span_a(qb, kc):
    return min(CH, (qb + 1) * P - kc * CH), kc == qb * P // CH


def span_b(qc, kb):
    q0 = max(qc * CH, kb * P)
    return q0, (qc + 1) * CH - q0, kb * P >= qc * CH


A_TILES = [(qb, kc, h0, nh) for qb in range(QB) for kc in range(qb * P // CH + 1)
           for h0, nh in heads_of_tiles(span_a(qb, kc)[0])]
B_STEPS = [(qc, kb) for qc in range(CHUNKS) for kb in range((qc + 1) * CH // P)]
B_TILES = [(s, h0, nh) for s, at in enumerate(B_STEPS) for h0, nh in heads_of_tiles(span_b(*at)[1])]
NA, NB, NBT = len(A_TILES), len(B_STEPS), len(B_TILES)
LAST_STEP = [max(i for i, (q, _) in enumerate(B_STEPS) if q == qc) for qc in range(CHUNKS)]
HOSTED = 11
NC = EXPERTS * FC
LAG = 3
RING = 4
MAX_SLOT = NA - HOSTED
SLOTS = 3
B_LAG = SLOTS - 1
SILU_AT = (1, 2, 5, 6)
INPUTS_AT = (3, 4, 5, 9, 15)
XP = 4
M_STEPS, SILU_STEPS = 5, 4
M_COLS = 2 * 3 * PAIRS * QB
V_TILES = [(0, 3), (3, 6), (6, 8)]
V_STEPS = 2 * len(V_TILES)
FIRST_ROUND = 11
PIECES = [(0, 4), (4, 8), (8, 16)]


def phase_1_order(first):
    tiles = list(range(0 if first else HOSTED, NA))
    order = []
    if first:
        order += [("max", i) for i in tiles[:FIRST_ROUND]]
        tiles = tiles[FIRST_ROUND:]
    for s in range(NC):
        order.append(("ffn", s))
        if not tiles and ("maxima", 0) not in order:
            order.append(("maxima", 0))
        if tiles:
            order.append(("max", tiles.pop(0)))
    return order


def build(nc, x, w_in, b_in, b_in_row, w_out, b_out, w_router, w_gate, w_up, w_down, out):
    q_scr = nc.dram_tensor("q_scratch", (B, P, NT, S), BF16).ap()
    k_scr = nc.dram_tensor("k_scratch", (B, P, NT, S), BF16).ap()
    inv_scr = nc.dram_tensor("inverse_sums_scratch", (B * CHUNKS, P, CH * H // P), F32).ap()
    raw_scr = nc.dram_tensor("weighted_values_scratch", (CHUNKS, UNITS, P, CH), F32).ap()
    ce_scr = nc.dram_tensor("combine_scratch", (EXPERTS, B * S), F32).ap()

    ctx = ExitStack()
    with ctx:
        def sb(name, shape, dt=F32):
            return ctx.enter_context(nc.sbuf_tensor(name, shape, dt))

        def sem(name):
            return ctx.enter_context(nc.semaphore(name))

        ps = ctx.enter_context(nc.psum_tensor("ps", [P, 8, CH], F32))

        x_sb = sb("x_sb", [P, TILES, E])
        xn_t = sb("xn_t", [P, B * S])
        w_in_sb = sb("w_in_sb", [P, 3 * E + EXPERTS])
        w_out_sb = sb("w_out_sb", [P, E])
        b_qk = sb("b_qk", [P, 2])
        b_v = sb("b_v", [P, E])
        b_o = sb("b_o", [P, 1])
        w_hi = [sb(f"w_hi{i}", [P, EXPERTS * DFF], F32R) for i in range(3)]
        w_lo = [sb(f"w_lo{i}", [P, EXPERTS * DFF], F32R) for i in range(3)]
        ident = sb("ident", [P, P])
        ident_h = sb("ident_h", [P, P], BF16)
        mask_q = sb("mask_q", [P, P], BF16)
        mask_k = sb("mask_k", [P, P], BF16)
        rank = sb("rank", [P, EXPERTS])
        q_a = sb("q_a", [P, PAIRS, S], BF16)
        k_a = sb("k_a", [P, PAIRS, 2, S], BF16)
        q_b = sb("q_b", [P, PAIRS, S], BF16)
        k_b = sb("k_b", [P, PAIRS, 2, S], BF16)
        v_all = sb("v_all", [P, UNITS, QB, G, VW])
        v_b = sb("v_b", [P, QB, G, VW])
        ce_b = sb("ce_b", [P, EXPERTS, TOK])
        xw = sb("xw", [P, EXPERTS, TOK])
        xw_hi = sb("xw_hi", [P, EXPERTS, TOK], F32R)
        xw_lo = sb("xw_lo", [P, EXPERTS, TOK], F32R)
        xc_hi = sb("xc_hi", [P, TOK], F32R)
        xc_lo = sb("xc_lo", [P, TOK], F32R)
        early = sb("early", [P, 3 * S])
        hid_hi = sb("hid_hi", [P, RING, TOK], F32R)
        hid_lo = sb("hid_lo", [P, RING, TOK], F32R)
        probs = sb("probs", [P, SLOTS, G, CH])
        mx = sb("mx", [P, CHUNKS, 2, PAIRS, QB])
        top_m = sb("top_m", [P, 2, PAIRS, QB])
        m_rest = sb("m_rest", [P, 2, PAIRS, QB])
        m_parts = sb("m_parts", [P, 2, 3, PAIRS, QB], BF16)
        m_t = sb("m_t", [M_COLS, P], BF16)
        rsum = sb("rsum", [P, 4, G])
        sum_c = sb("sum_c", [P, B * CHUNKS, CH * H // P])
        w_first = [sb(f"w_first{i}", [P, EXPERTS * DFF]) for i in range(2)]
        g_t = sb("g_t", [P, B * S])
        stat = sb("stat", [P, 8, TILES])
        warm = sb("warm", [P, 3])
        rs = sb("rs", [P, 8, TILES])
        ce_t = sb("ce_t", [P, P])

        parts_0 = early[:, :].bitcast(BF16).rearrange("p (i r s) -> p i r s", i=2, r=3)
        hid = early[:, 0:RING * TOK].rearrange("p (r t) -> p r t", t=TOK)
        gate = early[:, 4 * TOK:6 * TOK].rearrange("p (r t) -> p r t", t=TOK)
        silu_b = early[:, 6 * TOK:9 * TOK].rearrange("p (r t) -> p r t", t=TOK)
        raw_t = early[:, 9 * TOK:9 * TOK + CH]
        x_cur = early[:, 9 * TOK + CH:10 * TOK + CH]
        w_raw = [w_first[0][:, :], g_t[:, :], w_first[1][:, :]]
        pool_of = probs[:, :, :, :].rearrange("p a g c -> p (a g c)")
        rt = pool_of[:, 4 * S:5 * S].rearrange("p (r t e) -> p r t e", t=TILES, e=EXPERTS)
        ones_rows = pool_of[0:3, 5 * S:6 * S].bitcast(BF16)
        centre = [pool_of[:, 0:S], pool_of[:, 3 * S:4 * S]]
        parts_1 = pool_of[:, 0:3 * S].bitcast(BF16).rearrange("p (i r s) -> p i r s", i=2, r=3)
        parts = [parts_0, parts_1]
        square = ce_b[:, :, :].rearrange("p e t -> p (e t)")
        rest = xw[:, :, :].rearrange("p (r e) t -> p r (e t)", r=4)
        xw_f = xw[:, :, :].rearrange("p e t -> p (e t)")
        y_t = xw_f[:, CH:2 * CH]
        o_sb = [xw_f[:, (2 + i) * CH:(3 + i) * CH] for i in range(2)]
        ctx_in = [w_raw[2][:, i * CH:(i + 1) * CH] for i in range(B * CHUNKS)]
        sum_in = [w_raw[0][:, i * CH:(i + 1) * CH] for i in range(B * CHUNKS)]
        ctx_q = ce_b[:, 0:CH // TOK, :].rearrange("p e t -> p (e t)").rearrange("p (t e) -> p t e", e=E)
        v_flat = v_all[:, :, :, :, :].rearrange("p u k g s -> p (u k g s)")

        x_loaded = [sem(f"x_loaded{i}") for i in range(len(PIECES))]
        zero_ready = sem("zero_ready")
        proj_loaded = sem("proj_loaded")
        router_loaded = sem("router_loaded")
        w_loaded = [sem(f"w_loaded{i}") for i in range(3)]
        out_loaded = sem("out_loaded")
        masks_ready = sem("masks_ready")
        ones_ready = sem("ones_ready")
        warm_ready = sem("warm_ready")
        x_cur_loaded = sem("x_cur_loaded")
        ones_placed = sem("ones_placed")
        pool_step = sem("pool_step")
        dve_step = sem("dve_step")
        centred = sem("centred")
        squared = sem("squared")
        centred_last = sem("centred_last")
        squared_last = sem("squared_last")
        mean_ready = sem("mean_ready")
        var_ready = sem("var_ready")
        sd_ready = sem("sd_ready")
        xn_ready = sem("xn_ready")
        xn_turned = sem("xn_turned")
        xnt_ready = sem("xnt_ready")
        qk_done = sem("qk_done")
        v_done = sem("v_done")
        high_ready = sem("high_ready")
        rest_ready = sem("rest_ready")
        mid_ready = sem("mid_ready")
        low_ready = sem("low_ready")
        v_ready = sem("v_ready")
        w_hi_ready = sem("w_hi_ready")
        w_lo_ready = sem("w_lo_ready")
        scr_first = sem("scr_first")
        scr_others = sem("scr_others")
        scr_written = sem("scr_written")
        logits_cut = sem("logits_cut")
        router_exp = sem("router_exp")
        combine_ready = sem("combine_ready")
        combine_turned = sem("combine_turned")
        combine_copied = sem("combine_copied")
        combine_written = sem("combine_written")
        a_loaded = sem("a_loaded")
        b_loaded = sem("b_loaded")
        m_loaded = sem("m_loaded")
        ce_loaded = sem("ce_loaded")
        weighted = sem("weighted")
        x_hi_ready = sem("x_hi_ready")
        x_lo_ready = sem("x_lo_ready")
        a_scored = sem("a_scored")
        a_reduced = sem("a_reduced")
        m_step = sem("m_step")
        m_turned = sem("m_turned")
        m_copied = sem("m_copied")
        gu_done = sem("gu_done")
        relu_done = sem("relu_done")
        hid_ready = sem("hid_ready")
        hid_hi_ready = sem("hid_hi_ready")
        hid_lo_ready = sem("hid_lo_ready")
        ffn_done = sem("ffn_done")
        ez_done = sem("ez_done")
        silu_step = sem("silu_step")
        b_scored = sem("b_scored")
        exp_done = sem("exp_done")
        pv_done = sem("pv_done")
        raw_copied = sem("raw_copied")
        raw_stored = sem("raw_stored")
        ctx_loaded = [sem(f"ctx_loaded{c}") for c in range(B * CHUNKS)]
        sums_loaded = sem("sums_loaded")
        sums_inverted = sem("sums_inverted")
        inverse_stored = sem("inverse_stored")
        others_divided = sem("others_divided")
        tail_turned = sem("tail_turned")
        tail_step = sem("tail_step")
        ctxt_ready = sem("ctxt_ready")
        proj_done = sem("proj_done")
        y_ready = sem("y_ready")
        y_turned = sem("y_turned")
        o_ready = sem("o_ready")
        stored = [sem(f"stored{i}") for i in range(2)]

        block = ctx.enter_context(nc.Block())

        def gu_bank(s):
            return (2 if s in (12, 13) else 4) + s % 2

        def tile_view(bank, nh, w):
            if nh == G:
                return ps[:, bank:bank + 2, :].rearrange("p a c -> p (a c)")[:, 0:G * w]\
                    .rearrange("p (h w) -> p h w", w=w)
            return ps[:, bank:bank + 2, 0:w]

        def part(k, r):
            c, i = k // 2, k % 2
            return parts[c // CHUNKS][:, i, r, (c % CHUNKS) * CH:(c % CHUNKS + 1) * CH]

        def centre_of(i):
            t0, t1 = PIECES[i]
            b = t0 // QB
            return centre[b][:, (t0 - b * QB) * E:(t1 - b * QB) * E]

        def vr_place(t0, t1):
            w = E + EXPERTS
            k = (0, 1, 6)[t0 // 3]
            return ps[:, k, 0:(t1 - t0) * w].rearrange("p (t w) -> p t w", w=w)

        def qk_bank(k):
            return 2 + 2 * (k % 2) + k // 2 % 2

        @block.sync
        def _(sp):
            xv = x.rearrange("b (t p) e -> p (b t) e", p=P)

            def load_x(i):
                t0, t1 = PIECES[i]
                sp.dma_start(x_sb[:, t0:t1, :], xv[:, t0:t1, :]).then_inc(x_loaded[i], 16)

            for i in range(len(PIECES)):
                load_x(i)
            sp.dma_start(w_in_sb[:, 0:3 * E], w_in).then_inc(proj_loaded, 16)
            sp.dma_start(b_qk[:, :], b_in[:, 0:2]).then_inc(proj_loaded, 16)
            sp.dma_start(b_v[:, :], b_in_row[:, 2 * E:3 * E].to_broadcast([P, E])).then_inc(proj_loaded, 16)
            sp.dma_start(w_in_sb[:, 3 * E:3 * E + EXPERTS], w_router).then_inc(router_loaded, 16)
            for i, w in enumerate((w_gate.rearrange("e d f -> d e f"), w_up.rearrange("e d f -> d e f"),
                                   w_down.rearrange("e (c f) d -> f (e c) d", f=P))):
                sp.dma_start(w_raw[i].rearrange("p (a b) -> p a b", b=w.shape[2]), w).then_inc(w_loaded[i], 16)
            sp.dma_start(w_out_sb[:, :], w_out).then_inc(out_loaded, 16)
            sp.dma_start(b_o[:, :], b_out).then_inc(out_loaded, 16)

            def store_part(b, i, rows, run, done):
                first, count = (0, 3, 5)[run], (3, 2, 1)[run]
                src = (parts[b][rows, 0, run:run + 1, :].to_broadcast([rows.stop - rows.start, count, S])
                       if i == 0 else parts[b][rows, 1, 0:count, :])
                sp.dma_start((q_scr, k_scr)[i][b, rows, first:first + count, :], src).then_inc(done, 16)

            q_u = q_scr.rearrange("b (g a c d) t s -> (b g) c (d t) a s", g=GROUPS, a=PAIRS, c=2)
            k_u = k_scr.rearrange("b (g a c d) t s -> (b g) c (d t) a s", g=GROUPS, a=PAIRS, c=2)

            def load_qk(q_to, k_to, n, done):
                for hh in range(2):
                    r = slice(hh * HALF, hh * HALF + ROWS)
                    sp.dma_start(q_to[r, :, :], q_u[n, hh]).then_inc(done, 16)
                    sp.dma_start(k_to[r, :, hh, :], k_u[n, hh]).then_inc(done, 16)

            def load_ce(n):
                src = ce_scr[:, bass.ts(n, TOK)].unsqueeze(0).to_broadcast([P, EXPERTS, TOK])
                sp.dma_start(ce_b[:, :, :], src).then_inc(ce_loaded, 16)

            def load_x_cur(n):
                sp.dma_start(x_cur, xn_t[:, bass.ts(n, TOK)]).then_inc(x_cur_loaded, 16)

            def load_b(n):
                load_qk(q_b, k_b, n, b_loaded)
                sp.dma_start(v_b[:, :, :, :].rearrange("p k g s -> p (k g s)"),
                             v_flat[:, bass.ts(n, QB * G * VW)]).then_inc(b_loaded, 16)

            def load_m(n):
                sp.wait_ge(m_copied, n + 1)
                for hh in range(2):
                    r = hh * HALF + ROWS
                    sp.dma_start(q_b[r:r + 3, :, :].rearrange("r a (b q) -> r a b q", q=P),
                                 m_t[hh * M_COLS // 2:(hh + 1) * M_COLS // 2, :]).then_inc(m_loaded, 16)

            sp.wait_ge(high_ready, 4)
            store_part(0, 0, slice(0, G * D), 0, scr_first)
            store_part(0, 1, slice(0, G * D), 2, scr_first)
            sp.wait_ge(mid_ready, 4)
            store_part(0, 0, slice(0, G * D), 1, scr_first)
            store_part(0, 1, slice(0, G * D), 1, scr_first)
            sp.wait_ge(low_ready, 4)
            store_part(0, 1, slice(0, G * D), 0, scr_first)
            store_part(0, 0, slice(0, G * D), 2, scr_first)
            for run in range(3):
                store_part(0, 0, slice(G * D, P), run, scr_others)
            sp.wait_ge(scr_first, 16 * NT)
            sp.wait_ge(zero_ready, 2)
            load_qk(q_a, k_a, 0, a_loaded)
            for run in range(3):
                store_part(0, 1, slice(G * D, P), run, scr_others)
            sp.wait_ge(combine_copied, 1)
            sp.dma_start(ce_scr.rearrange("e (t k) -> (e t) k", k=P), ce_t[:, :]).then_inc(combine_written, 16)
            sp.wait_ge(combine_written, 16)
            load_ce(0)
            sp.wait_ge(ones_ready, 1)
            sp.wait_ge(zero_ready, 4)
            for hh in range(2):
                r = hh * HALF + ROWS
                sp.dma_start(k_b[r:r + 3, :, hh, :], ones_rows[:, :].rearrange("r (a s) -> r a s", a=2))\
                  .then_inc(ones_placed, 16)
            sp.wait_ge(v_ready, V_STEPS)
            load_b(0)
            sp.wait_ge(low_ready, 8)
            for i in range(2):
                for run in range(3):
                    store_part(1, i, slice(0, P), run, scr_written)
            sp.wait_ge(v_ready, B * V_STEPS)
            sp.wait_ge(scr_written, 16 * NT)
            sp.wait_ge(scr_others, 16 * NT)
            sp.wait_ge(a_scored, NA)
            load_qk(q_a, k_a, 1, a_loaded)
            load_m(0)

            def store_raw(n, qc):
                sp.wait_ge(raw_copied, n * CHUNKS + qc + 1)
                sp.dma_start(raw_scr[qc, n], raw_t).then_inc(raw_stored, 16)

            def load_ctx(c, units=GROUPS):
                b, qc = c // CHUNKS, c % CHUNKS
                sp.wait_ge(raw_stored, 16 * (1 + (b * GROUPS + units - 1) * CHUNKS + qc + 1))
                slots = raw_scr[qc, b * GROUPS:b * GROUPS + units].rearrange("u (g s) q -> (u g) s q", s=SLOT)
                rows, heads = slice(0, units * G * D), units * G
                sp.dma_start(ctx_in[c][rows, :], slots[:, 0:D, :]).then_inc(ctx_loaded[c], 16)
                if c == 2:
                    sp.dma_start(sum_in[c][rows, :], slots[:, D:D + 1, :].to_broadcast([heads, D, CH]))\
                      .then_inc(ctx_loaded[c], 16)
                else:
                    sp.dma_start(sum_c[0:heads * D, c, :], slots[:, D, :].rearrange("h (a q) -> h a q", a=D))\
                      .then_inc(sums_loaded, 16)

            def store_inverse(c):
                units = GROUPS - (c == B * CHUNKS - 1)
                rows = slice(0, units * G * D)
                sp.wait_ge(sums_inverted, 1 if c < CHUNKS else 2)
                sp.dma_start(inv_scr[c, rows, :], sum_c[rows, c, :]).then_inc(inverse_stored, 16)

            def load_inverse(c):
                units = GROUPS - (c == B * CHUNKS - 1)
                rows, heads = slice(0, units * G * D), units * G
                sp.wait_ge(inverse_stored, 48)
                src = inv_scr[c, rows, :].rearrange("(h a) q -> h (a q)", a=D).unsqueeze(1)
                sp.dma_start(sum_in[c][rows, :], src.to_broadcast([heads, D, CH])).then_inc(ctx_loaded[c], 16)

            def unit_loads(n, following):
                sp.wait_ge(weighted, n * XP)
                load_ce(n)
                load_x_cur(n)
                store_raw(n - 1, 0)
                sp.wait_ge(pv_done, n * NB)
                load_b(n)
                store_raw(n - 1, 1)
                if following:
                    sp.wait_ge(a_scored, n * NA + NA)
                    load_qk(q_a, k_a, n + 1, a_loaded)
                load_m(n)

            with sp.Fori(1, UNITS - 1) as n:
                unit_loads(n, True)
            load_ctx(0)
            load_ctx(1)
            unit_loads(UNITS - 1, False)
            ov = out.rearrange("b (t p) e -> p (b t) e", p=P)

            def store_out(c):
                sp.wait_ge(o_ready, c + 1)
                sp.dma_start(ov[:, 4 * c:4 * c + 4, :], o_sb[c % 2].rearrange("p (t e) -> p t e", e=E))\
                  .then_inc(stored[c % 2], 16)

            load_ctx(B * CHUNKS - 1, GROUPS - 1)
            for c in (0, 1, B * CHUNKS - 1):
                store_inverse(c)
            for c in (0, 1, B * CHUNKS - 1):
                load_inverse(c)
            store_raw(UNITS - 1, 0)
            load_ctx(2)
            for c in range(B * CHUNKS):
                store_out(c)
            for i in range(2):
                sp.wait_ge(stored[i], 16 * B * CHUNKS // 2)

        @block.gpsimd
        def _(pool):
            for m in (ident, ident_h, mask_q):
                nc.gpsimd.memset(m[:, :], 0.0)
            nc.gpsimd.memset(mask_k[:, :], 0.0).then_inc(pool_step, 1)
            pool.wait_ge(pool_step, 1)
            for m in (ident, ident_h):
                nc.gpsimd.affine_select(out=m[:, :], in_=m[:, :], compare_op=ALU.not_equal, fill=1.0, base=0,
                                        pattern=[[-1, P]], channel_multiplier=1)
            nc.gpsimd.affine_select(out=mask_q[:, :], in_=mask_q[:, :], compare_op=ALU.is_ge, fill=MASKED, base=0,
                                    pattern=[[-1, P]], channel_multiplier=1)
            nc.gpsimd.affine_select(out=mask_k[:, :], in_=mask_k[:, :], compare_op=ALU.is_ge, fill=MASKED,
                                    base=0, pattern=[[1, P]], channel_multiplier=-1).then_inc(masks_ready, 1)
            nc.gpsimd.memset(ones_rows[:, :], 1.0).then_inc(ones_ready, 1)
            nc.gpsimd.memset(q_a[:, :, :].bitcast(F32), 0.0).then_inc(zero_ready, 1)
            nc.gpsimd.memset(k_a[:, :, :, :].bitcast(F32), 0.0).then_inc(zero_ready, 1)
            t = slice(PIECES[-1][0] * E, PIECES[-1][1] * E)
            xc = centre_of(len(PIECES) - 1).rearrange("p (t e) -> p t e", e=E)
            pool.wait_ge(x_loaded[-1], 16)
            pool.wait_ge(mean_ready, 1)
            nc.gpsimd.tensor_tensor(xc, x_sb[:, PIECES[-1][0]:, :],
                                    stat[:, 0, PIECES[-1][0]:].unsqueeze(2).to_broadcast([P, xc.shape[1], E]),
                                    ALU.subtract).then_inc(centred_last, 1)
            pool.wait_ge(centred_last, 1)
            last = centre_of(len(PIECES) - 1)
            nc.gpsimd.tensor_tensor(square[:, t], last, last, ALU.mult).then_inc(squared_last, 1)

            def low_parts(b):
                for k in range(4 * b, 4 * b + 4):
                    pool.wait_ge(mid_ready, k + 1)
                    nc.gpsimd.tensor_tensor(part(k, 2), rest[:, k % 4, :], part(k, 1), ALU.subtract)\
                      .then_inc(low_ready, 1)

            def weights_low(i):
                pool.wait_ge(w_hi_ready, i + 1)
                nc.gpsimd.tensor_tensor(w_lo[i][:, :], w_raw[i], w_hi[i][:, :].bitcast(F32), ALU.subtract)\
                  .then_inc(w_lo_ready, 1)

            weights_low(0)
            low_parts(0)
            weights_low(1)
            weights_low(2)
            nc.gpsimd.memset(q_b[:, :, :].bitcast(F32), 0.0).then_inc(zero_ready, 1)
            nc.gpsimd.memset(k_b[:, :, :, :].bitcast(F32), 0.0).then_inc(zero_ready, 1)
            low_parts(1)

            def piece(i):
                return slice(i * EXPERTS // XP, (i + 1) * EXPERTS // XP)

            def weigh_inputs(i, x_of):
                nc.gpsimd.tensor_tensor(xw[:, piece(i), :], ce_b[:, piece(i), :],
                                        x_of.unsqueeze(1).to_broadcast([P, EXPERTS // XP, TOK]), ALU.mult)\
                  .then_inc(weighted, 1)

            def low_tokens(n, x_of):
                pool.wait_ge(x_hi_ready, n * (XP + 1) + 1)
                nc.gpsimd.tensor_tensor(xc_lo[:, :], x_of, xc_hi[:, :].bitcast(F32), ALU.subtract)\
                  .then_inc(x_lo_ready, 1)

            def low_inputs(n, i):
                pool.wait_ge(x_hi_ready, n * (XP + 1) + i + 2)
                nc.gpsimd.tensor_tensor(xw_lo[:, piece(i), :], xw[:, piece(i), :],
                                        xw_hi[:, piece(i), :].bitcast(F32), ALU.subtract)\
                  .then_inc(x_lo_ready, 1)

            def hidden_low(n, s):
                pool.wait_ge(hid_hi_ready, n * NC + s + 1)
                nc.gpsimd.tensor_tensor(hid_lo[:, s % RING, :], hid[:, s % RING, :],
                                        hid_hi[:, s % RING, :].bitcast(F32), ALU.subtract)\
                  .then_inc(hid_lo_ready, 1)

            x_first = xn_t[:, 0:TOK]
            pool.wait_ge(low_ready, 4 * B)
            pool.wait_ge(ce_loaded, 16)
            weigh_inputs(0, x_first)
            low_tokens(0, x_first)
            low_inputs(0, 0)
            weigh_inputs(1, x_first)
            low_inputs(0, 1)
            for s in range(NC):
                if s in (2, 6):
                    weigh_inputs(s // 4 + 2, x_first)
                if s in (4, 8):
                    low_inputs(0, s // 4 + 1)
                hidden_low(0, s)
            with pool.Fori(1, UNITS) as n:
                pool.wait_ge(gu_done, n * NC)
                pool.wait_ge(ce_loaded, n * 16 + 16)
                pool.wait_ge(x_cur_loaded, n * 16)
                weigh_inputs(0, x_cur)
                low_tokens(n, x_cur)
                for i in range(XP):
                    if i + 1 < XP:
                        weigh_inputs(i + 1, x_cur)
                    low_inputs(n, i)
                for s in range(NC):
                    hidden_low(n, s)

        @block.scalar
        def _(act):
            def squares(i):
                t = slice(PIECES[i][0] * E, PIECES[i][1] * E)
                act.wait_ge(centred, i + 1)
                nc.scalar.activation(square[:, t], centre_of(i), ACT.Square).then_inc(squared, 1)

            def deviation(i):
                t = slice(*PIECES[i])
                act.wait_ge(var_ready, i + 1)
                nc.scalar.activation(stat[:, 2, t], stat[:, 1, t], ACT.Sqrt).then_inc(sd_ready, 1)

            def turned_x(c):
                act.wait_ge(xn_turned, (1, 2, 4, 3)[c])
                nc.scalar.activation(xn_t[:, c * CH:(c + 1) * CH], ps[:, 6 + c % 2, :], ACT.Copy).then_inc(xnt_ready, 1)

            def high(k):
                if k == 0:
                    act.wait_ge(proj_loaded, 48)
                act.wait_ge(qk_done, k + 1)
                nc.scalar.activation(part(k, 0), ps[:, qk_bank(k), :], ACT.Identity, bias=b_qk[:, k % 2:k % 2 + 1])\
                  .then_inc(high_ready, 1)

            def mid(k):
                act.wait_ge(rest_ready, k + 1)
                nc.scalar.activation(part(k, 1), rest[:, k % 4, :], ACT.Copy).then_inc(mid_ready, 1)

            def weights_high(i):
                act.wait_ge(w_loaded[i], 16)
                nc.scalar.activation(w_hi[i][:, :], w_raw[i], ACT.Copy).then_inc(w_hi_ready, 1)

            act.wait_ge(warm_ready, 1)
            nc.scalar.activation(warm[:, 2:3], warm[:, 0:1], ACT.Sqrt)
            squares(0)
            squares(1)
            deviation(0)
            deviation(1)
            weights_high(0)
            turned_x(0)
            turned_x(1)
            deviation(2)
            nc.scalar.activation(warm[:, 2:3], warm[:, 0:1], ACT.Exp)
            high(0)
            high(1)
            high(2)
            mid(0)
            high(3)
            mid(1)
            turned_x(3)
            turned_x(2)
            mid(2)
            mid(3)
            weights_high(1)
            weights_high(2)
            act.wait_ge(logits_cut, 1)
            nc.scalar.activation(rt[:, 1, :, :], rt[:, 0, :, :], ACT.Exp).then_inc(router_exp, 1)
            for k in range(4, 8):
                high(k)
            act.wait_ge(combine_turned, 1)
            nc.scalar.activation(ce_t[:, :], ps[:, 6, 0:P], ACT.Copy).then_inc(combine_copied, 1)
            for k in range(4, 8):
                mid(k)

            def hidden_high(n, s):
                act.wait_ge(hid_ready, n * NC + s + 1)
                nc.scalar.activation(hid_hi[:, s % RING, :], hid[:, s % RING, :], ACT.Copy)\
                  .then_inc(hid_hi_ready, 1)

            def inputs_high(n, i, first=False):
                if i == 0:
                    if not first:
                        act.wait_ge(x_cur_loaded, n * 16)
                    nc.scalar.activation(xc_hi[:, :], xn_t[:, 0:TOK] if first else x_cur, ACT.Copy)\
                      .then_inc(x_hi_ready, 1)
                else:
                    e = slice((i - 1) * EXPERTS // XP, i * EXPERTS // XP)
                    act.wait_ge(weighted, n * XP + i)
                    nc.scalar.activation(xw_hi[:, e, :], xw[:, e, :], ACT.Copy).then_inc(x_hi_ready, 1)

            def phase_1(n, first):
                order = phase_1_order(first)
                turn_at = order.index(("maxima", 0))
                for at, (what, s) in enumerate(order):
                    if what == "ffn":
                        if first and s == 0:
                            for k in range(3):
                                inputs_high(n, k, True)
                        act.wait_ge(gu_done, n * NC + s + 1)
                        nc.scalar.activation(gate[:, s % 2, :], ps[:, gu_bank(s), 0:TOK], ACT.Relu)\
                          .then_inc(relu_done, 1)
                        if s >= 1:
                            hidden_high(n, s - 1)
                        if first and s in (3, 7):
                            inputs_high(n, s // 4 + 3, True)
                    if at == turn_at + 3:
                        act.wait_ge(m_turned, n + 1)
                        nc.scalar.activation(m_t[:, :], ps[0:M_COLS, 6, 0:P // 2].bitcast(BF16), ACT.Copy)\
                          .then_inc(m_copied, 1)
                hidden_high(n, NC - 1)

            def phase_2(n, following):
                for i, (s, h0, nh) in enumerate(B_TILES):
                    w = span_b(*B_STEPS[s])[1]
                    act.wait_ge(b_scored, n * NBT + i + 1)
                    nc.scalar.activation(probs[:, s % SLOTS, h0:h0 + nh, 0:w],
                                         tile_view(2 * (i % 2), nh, w), ACT.Exp, scale=SCALE).then_inc(exp_done, 1)
                    if following is not None and i in INPUTS_AT:
                        inputs_high(following, INPUTS_AT.index(i))
                    if i == 3:
                        act.wait_ge(ffn_done, n + 1)
                        nc.scalar.activation(silu_b[:, 0, :], ps[:, 7, 0:TOK], ACT.Exp, scale=-1.0)\
                          .then_inc(ez_done, 1)

            act.wait_ge(scr_others, 16 * NT)
            phase_1(0, True)
            act.wait_ge(scr_written, 16 * NT)
            with act.Fori(1, UNITS) as n:
                phase_2(n - 1, n)
                phase_1(n, False)
            phase_2(UNITS - 1, None)

        @block.vector
        def _(dve):
            steps = [0]

            def link(ins):
                steps[0] += 1
                ins.then_inc(dve_step, 1)
                dve.wait_ge(dve_step, steps[0])

            def centre_x(i):
                t, m = slice(*PIECES[i]), PIECES[i][1] - PIECES[i][0]
                dve.wait_ge(x_loaded[i], 16)
                link(nc.vector.tensor_reduce(stat[:, 0, t], x_sb[:, t, :], X, ALU.add))
                mean = nc.vector.tensor_scalar(stat[:, 0, t], stat[:, 0, t], 1.0 / E, None, ALU.mult)
                if i == len(PIECES) - 1:
                    mean.then_inc(mean_ready, 1)
                    return
                link(mean)
                xc = centre_of(i).rearrange("p (t e) -> p t e", e=E)
                nc.vector.tensor_tensor(xc, x_sb[:, t, :],
                                        stat[:, 0, t].unsqueeze(2).to_broadcast([P, m, E]), ALU.subtract)\
                  .then_inc(centred, 1)

            def variance(i):
                t = slice(*PIECES[i])
                if i < len(PIECES) - 1:
                    dve.wait_ge(squared, i + 1)
                else:
                    dve.wait_ge(squared_last, 1)
                link(nc.vector.tensor_reduce(stat[:, 1, t], square_t[:, t, :], X, ALU.add))
                nc.vector.tensor_scalar(stat[:, 1, t], stat[:, 1, t], 1.0 / E, EPS, ALU.mult, ALU.add)\
                  .then_inc(var_ready, 1)

            def normalise(i):
                t, m = slice(*PIECES[i]), PIECES[i][1] - PIECES[i][0]
                dve.wait_ge(sd_ready, i + 1)
                link(nc.vector.reciprocal(stat[:, 3, t], stat[:, 2, t]))
                link(nc.vector.tensor_tensor(stat[:, 4, t], stat[:, 3, t], stat[:, 3, t], ALU.mult))
                link(nc.vector.tensor_tensor(stat[:, 5, t], stat[:, 4, t], stat[:, 1, t], ALU.mult))
                link(nc.vector.tensor_scalar(stat[:, 6, t], stat[:, 5, t], -0.5, 1.5, ALU.mult, ALU.add))
                link(nc.vector.tensor_tensor(stat[:, 7, t], stat[:, 6, t], stat[:, 3, t], ALU.mult))
                xc = centre_of(i).rearrange("p (t e) -> p t e", e=E)
                nc.vector.tensor_tensor(xc, xc, stat[:, 7, t].unsqueeze(2).to_broadcast([P, m, E]), ALU.mult)\
                  .then_inc(xn_ready, 1)

            def rest_of(k):
                if k == 0:
                    dve.wait_ge(proj_loaded, 48)
                dve.wait_ge(high_ready, k + 1)
                if k >= 4:
                    dve.wait_ge(low_ready, k - 3)
                nc.vector.scalar_tensor_tensor(out=rest[:, k % 4, :], in0=ps[:, qk_bank(k), :],
                                               scalar=b_qk[:, k % 2:k % 2 + 1], in1=part(k, 0),
                                               op0=ALU.add, op1=ALU.subtract).then_inc(rest_ready, 1)

            def values(b):
                for j, (t0, t1) in enumerate(V_TILES):
                    dve.wait_ge(v_done, len(V_TILES) * b + j + 1)
                    nc.vector.tensor_copy(rt[:, 0, b * QB + t0:b * QB + t1, :], vr_place(t0, t1)[:, :, E:])\
                      .then_inc(v_ready, 1)
                    split = "p t (g h d) -> p g t h d"
                    nc.vector.tensor_tensor(
                        v_all[:, b * GROUPS:(b + 1) * GROUPS, t0:t1, :, 0:D],
                        vr_place(t0, t1)[:, :, 0:E].rearrange(split, g=GROUPS, d=D),
                        b_v[:, :].unsqueeze(1).to_broadcast([P, t1 - t0, E]).rearrange(split, g=GROUPS, d=D),
                        ALU.add).then_inc(v_ready, 1)

            def wide(a):
                return a.unsqueeze(2).to_broadcast([P, TILES, EXPERTS])

            def router():
                rank_w = rank[:, :].unsqueeze(1).to_broadcast([P, TILES, EXPERTS])
                dve.wait_ge(v_ready, B * V_STEPS)
                lg = rt[:, 0, :, :]
                link(nc.vector.tensor_reduce(rs[:, 0, :], lg, X, ALU.max))
                nc.vector.tensor_tensor(lg, lg, wide(rs[:, 0, :]), ALU.subtract).then_inc(logits_cut, 1)
                dve.wait_ge(router_exp, 1)
                p = rt[:, 1, :, :]
                link(nc.vector.tensor_reduce(rs[:, 1, :], p, X, ALU.max))

                def first_of(v, top, eq, key, at, mask):
                    link(nc.vector.tensor_tensor(rt[:, eq, :, :], v, wide(rs[:, top, :]), ALU.is_equal))
                    link(nc.vector.tensor_tensor(rt[:, key, :, :], rt[:, eq, :, :], rank_w, ALU.mult))
                    link(nc.vector.tensor_reduce(rs[:, at, :], rt[:, key, :, :], X, ALU.max))
                    link(nc.vector.tensor_tensor(rt[:, mask, :, :], rt[:, key, :, :], wide(rs[:, at, :]),
                                                 ALU.is_equal))

                first_of(p, 1, 2, 3, 2, 4)
                link(nc.vector.scalar_tensor_tensor(out=rt[:, 5, :, :], in0=rt[:, 4, :, :], scalar=-2.0, in1=p,
                                                    op0=ALU.mult, op1=ALU.add))
                link(nc.vector.tensor_reduce(rs[:, 3, :], rt[:, 5, :, :], X, ALU.max))
                first_of(rt[:, 5, :, :], 3, 2, 3, 4, 6)
                link(nc.vector.tensor_tensor(rs[:, 5, :], rs[:, 1, :], rs[:, 3, :], ALU.add))
                nc.vector.tensor_tensor(rt[:, 7, :, :], rt[:, 4, :, :], rt[:, 6, :, :], ALU.add)
                link(nc.vector.reciprocal(rs[:, 6, :], rs[:, 5, :]))
                link(nc.vector.tensor_tensor(rt[:, 2, :, :], rt[:, 7, :, :], p, ALU.mult))
                nc.vector.tensor_tensor(
                    rt[:, 3, :, :].rearrange("p t e -> p (t e)").rearrange("p (e t) -> p t e", t=TILES),
                    rt[:, 2, :, :], wide(rs[:, 6, :]), ALU.mult).then_inc(combine_ready, 1)

            square_t = square.rearrange("p (t e) -> p t e", e=E)
            nc.vector.memset(warm[:, 0:1], 1.0).then_inc(warm_ready, 1)
            nc.vector.memset(warm[:, 1:2], 1.0).then_inc(raw_stored, 16)
            for e in range(EXPERTS):
                nc.vector.memset(rank[:, e:e + 1], float(EXPERTS - e))
            nc.vector.memset(v_all[:, :, :, :, D:VW], 1.0)
            link(nc.vector.memset(mx[:, :, :, :, :], 4 * MASKED))
            centre_x(0)
            centre_x(1)
            centre_x(2)
            variance(0)
            variance(1)
            normalise(0)
            normalise(1)
            variance(2)
            normalise(2)
            for k in range(4):
                rest_of(k)
            values(0)
            values(1)
            router()
            for k in range(4, 8):
                rest_of(k)

            def raw_copy(n, qc):
                dve.wait_ge(pv_done, n * NB + LAST_STEP[qc] + 1)
                dve.wait_ge(raw_stored, 16 * (n * CHUNKS + qc + 1))
                nc.vector.tensor_copy(raw_t, ps[:, 6, :]).then_inc(raw_copied, 1)

            def reduce_tile(n, i, bank):
                qb, kc, h0, nh = A_TILES[i]
                w, _ = span_a(qb, kc)
                dve.wait_ge(a_scored, n * NA + i + 1)
                src = tile_view(bank, nh, w).rearrange("p (a c) w -> p a c w", c=2)
                dst = mx[:, kc, :, h0 // 2:(h0 + nh) // 2, qb].rearrange("p c a -> p a c")
                nc.vector.tensor_reduce(dst, src, X, ALU.max).then_inc(a_reduced, 1)

            def hidden(n, s):
                dve.wait_ge(relu_done, n * NC + s + 1)
                nc.vector.tensor_tensor(hid[:, s % RING, :], gate[:, s % 2, :], ps[:, gu_bank(s), TOK:2 * TOK],
                                        ALU.mult).then_inc(hid_ready, 1)

            def split_max(n):
                dve.wait_ge(a_reduced, n * NA + NA)
                at = n * M_STEPS
                nc.vector.tensor_tensor(top_m[:, :, :, :], mx[:, 0], mx[:, 1], ALU.max).then_inc(m_step, 1)
                dve.wait_ge(m_step, at + 1)
                nc.vector.tensor_scalar(m_parts[:, :, 0], top_m[:, :, :, :], -1.0, None, ALU.mult).then_inc(m_step, 1)
                dve.wait_ge(m_step, at + 2)
                nc.vector.scalar_tensor_tensor(out=m_rest[:, :, :, :], in0=top_m[:, :, :, :], scalar=-1.0,
                                               in1=m_parts[:, :, 0], op0=ALU.mult, op1=ALU.subtract)\
                  .then_inc(m_step, 1)
                dve.wait_ge(m_step, at + 3)
                nc.vector.tensor_copy(m_parts[:, :, 1], m_rest[:, :, :, :]).then_inc(m_step, 1)
                dve.wait_ge(m_step, at + 4)
                nc.vector.tensor_tensor(m_parts[:, :, 2], m_rest[:, :, :, :], m_parts[:, :, 1], ALU.subtract)\
                  .then_inc(m_step, 1)

            def silu(n, step):
                at = n * SILU_STEPS
                if step == 0:
                    dve.wait_ge(ez_done, n + 1)
                    nc.vector.tensor_scalar(silu_b[:, 1, :], silu_b[:, 0, :], 1.0, None, ALU.add)\
                      .then_inc(silu_step, 1)
                elif step < 3:
                    half = slice((step - 1) * TOK // 2, step * TOK // 2)
                    dve.wait_ge(silu_step, at + 1)
                    nc.vector.reciprocal(silu_b[:, 2, half], silu_b[:, 1, half]).then_inc(silu_step, 1)
                else:
                    dve.wait_ge(silu_step, at + 3)
                    nc.vector.tensor_tensor(g_t[:, bass.ts(n, TOK)], ps[:, 7, 0:TOK], silu_b[:, 2, :], ALU.mult)\
                      .then_inc(silu_step, 1)

            def invert_sums():
                dve.wait_ge(sums_loaded, 48)
                nc.vector.reciprocal(sum_c[:, 0:CHUNKS, :], sum_c[:, 0:CHUNKS, :]).then_inc(sums_inverted, 1)
                nc.vector.reciprocal(sum_c[0:OTHERS, B * CHUNKS - 1, :], sum_c[0:OTHERS, B * CHUNKS - 1, :]).then_inc(sums_inverted, 1)

            def divided(c, rows=slice(0, P)):
                dve.wait_ge(ctx_loaded[c], 32)
                if c == 2:
                    nc.vector.reciprocal(sum_in[c][rows, :], sum_in[c][rows, :]).then_inc(sums_inverted, 1)
                    dve.wait_ge(sums_inverted, 3)
                nc.vector.tensor_tensor(ctx_in[c][rows, :], ctx_in[c][rows, :], sum_in[c][rows, :], ALU.mult)\
                  .then_inc(ctxt_ready if rows.stop == P else others_divided, 1)

            def divided_tail():
                dve.wait_ge(tail_turned, 1)
                raw = ps[:, 7, :].rearrange("p (t g s) -> p t g s", t=4, s=SLOT)
                nc.vector.reciprocal(rsum[:, :, :], raw[:, :, :, D]).then_inc(tail_step, 1)
                dve.wait_ge(tail_step, 1)
                nc.vector.tensor_tensor(ctx_q[:, :, OTHERS:].rearrange("p t (g d) -> p t g d", g=G),
                                        raw[:, :, :, 0:D], rsum[:, :, :].unsqueeze(3).to_broadcast([P, 4, G, D]),
                                        ALU.mult).then_inc(tail_step, 1)
                dve.wait_ge(tail_turned, 2)
                nc.vector.tensor_copy(ctx_in[-1][OTHERS:, :], ps[OTHERS:, 6, :]).then_inc(ctxt_ready, 1)

            def gated(c):
                dve.wait_ge(proj_done, c + 1)
                if c == 0:
                    dve.wait_ge(out_loaded, 32)
                dve.wait_ge(silu_step, ((c + 1) * CH // TOK) * SILU_STEPS)
                nc.vector.scalar_tensor_tensor(out=y_t, in0=ps[:, 4, :], scalar=b_o[:, 0:1],
                                               in1=g_t[:, c * CH:(c + 1) * CH], op0=ALU.add, op1=ALU.mult)\
                  .then_inc(y_ready, 1)

            def residual(c):
                dve.wait_ge(y_turned, c + 1)
                if c >= 2:
                    dve.wait_ge(stored[c % 2], 16 * (c // 2))
                nc.vector.tensor_tensor(o_sb[c % 2], ps[:, 5, :],
                                        x_sb[:, 4 * c:4 * c + 4, :].rearrange("p t e -> p (t e)"), ALU.add)\
                  .then_inc(o_ready, 1)

            def phase_1(n, first):
                for at, (what, i) in enumerate(phase_1_order(first)):
                    if what == "max":
                        reduce_tile(n, i, 2 * (i % 2))
                    elif what == "ffn":
                        if first or i:
                            hidden(n, i)
                    else:
                        split_max(n)

            def phase_2(n, following):
                for s in range(HOSTED):
                    reduce_tile(following, s, 4)
                    if s == LAST_STEP[0] + B_LAG - 1:
                        raw_copy(n, 0)
                    if s in SILU_AT:
                        silu(n, SILU_AT.index(s))
                raw_copy(n, CHUNKS - 1)
                hidden(following, 0)

            phase_1(0, True)
            with dve.Fori(1, UNITS) as n:
                phase_2(n - 1, n)
                phase_1(n, False)
            invert_sums()
            for step in range(SILU_STEPS):
                silu(UNITS - 1, step)
            divided(0)
            divided(1)
            divided(B * CHUNKS - 1, slice(0, OTHERS))
            raw_copy(UNITS - 1, 0)
            gated(0)
            residual(0)
            divided(2)
            gated(1)
            residual(1)
            raw_copy(UNITS - 1, 1)
            gated(2)
            divided_tail()
            residual(2)
            gated(3)
            residual(3)

        @block.tensor
        def _(pe):
            def turn_x(c):
                pe.wait_ge(xn_ready, min(c, len(PIECES) - 1) + 1)
                if c >= 2:
                    pe.wait_ge(xnt_ready, 2)
                for t in range(4):
                    at = c % CHUNKS * CH + t * E
                    mm = nc.tensor.transpose(ps[:, 6 + c % 2, t * P:(t + 1) * P],
                                             centre[c // CHUNKS][:, at:at + E], ident[:, :])
                mm.then_inc(xn_turned, 1)

            def project_qk(c):
                pe.wait_ge(xnt_ready, c + 1)
                for k in (2 * c, 2 * c + 1):
                    if k >= 4:
                        pe.wait_ge(rest_ready, k - 3)
                    nc.tensor.matmul(ps[:, qk_bank(k), :], w_in_sb[:, (k % 2) * E:(k % 2 + 1) * E],
                                     xn_t[:, c * CH:(c + 1) * CH], start=True, stop=True).then_inc(qk_done, 1)

            def project_v(b):
                for j, (t0, t1) in enumerate(V_TILES):
                    if b:
                        pe.wait_ge(v_ready, 2 * j + 2)
                    for t in range(t0, t1):
                        mm = nc.tensor.matmul(vr_place(t0, t1)[:, t - t0, :],
                                              xn_t[:, b * S + t * P:b * S + (t + 1) * P], w_in_sb[:, 2 * E:],
                                              start=True, stop=True)
                    mm.then_inc(v_done, 1)

            pe.wait_ge(masks_ready, 1)
            turn_x(0)
            turn_x(1)
            pe.wait_ge(proj_loaded, 48)
            project_qk(0)
            project_qk(1)
            pe.wait_ge(router_loaded, 16)
            turn_x(3)
            turn_x(2)
            pe.wait_ge(xnt_ready, 4)
            project_v(0)
            project_v(1)
            project_qk(2)
            project_qk(3)

            pe.wait_ge(combine_ready, 1)
            nc.tensor.transpose(ps[:, 6, 0:P], rt[:, 3, :, :].rearrange("p t e -> p (t e)"), ident[:, :])\
              .then_inc(combine_turned, 1)

            def three(out_ap, hi, lo, x_hi, x_lo, start=True, stop=True):
                nc.tensor.matmul(out_ap, hi, x_hi, start=start, stop=False)
                nc.tensor.matmul(out_ap, hi, x_lo, start=False, stop=False)
                return nc.tensor.matmul(out_ap, lo, x_hi, start=False, stop=stop)

            def gate_up(n, s):
                e, c = s // FC, s % FC
                if c == 0 and e % (EXPERTS // XP) == 0:
                    pe.wait_ge(x_lo_ready, n * (XP + 1) + e * XP // EXPERTS + 2)
                f = slice(e * DFF + c * P, e * DFF + (c + 1) * P)
                k = gu_bank(s)
                before = [t for t in range(s) if gu_bank(t) == k]
                if before:
                    pe.wait_ge(hid_ready, n * NC + before[-1] + 1)
                three(ps[:, k, 0:TOK], w_hi[0][:, f], w_lo[0][:, f], xc_hi[:, :], xc_lo[:, :])
                three(ps[:, k, TOK:2 * TOK], w_hi[1][:, f], w_lo[1][:, f], xw_hi[:, e, :], xw_lo[:, e, :])\
                    .then_inc(gu_done, 1)

            def down(n, s):
                pe.wait_ge(hid_lo_ready, n * NC + s + 1)
                f = slice(s * E, (s + 1) * E)
                mm = three(ps[:, 7, 0:TOK], w_hi[2][:, f], w_lo[2][:, f], hid_hi[:, s % RING, :],
                           hid_lo[:, s % RING, :], start=(s == 0), stop=(s == NC - 1))
                if s == NC - 1:
                    mm.then_inc(ffn_done, 1)

            def score(bank, h0, nh, w, stationary, moving, mask_at, mask):
                view = tile_view(bank, nh, w)
                for h in range(nh):
                    mm = nc.tensor.matmul(view[:, h, :], stationary(h0 + h), moving(h0 + h),
                                          start=True, stop=mask_at is None)
                    if mask_at is not None:
                        mm = nc.tensor.matmul(view[:, h, mask_at:mask_at + P], ident_h[:, :], mask[:, :],
                                              start=False, stop=True)
                return mm

            def score_a(n, i, bank):
                qb, kc, h0, nh = A_TILES[i]
                w, diagonal = span_a(qb, kc)
                score(bank, h0, nh, w, lambda h: q_a[:, h // 2, qb * P:(qb + 1) * P],
                      lambda h: k_a[:, h // 2, h % 2, kc * CH:kc * CH + w],
                      w - P if diagonal else None, mask_q).then_inc(a_scored, 1)

            def score_b(n, i):
                s, h0, nh = B_TILES[i]
                q0, w, diagonal = span_b(*B_STEPS[s])
                kb = B_STEPS[s][1]
                if i >= 2:
                    pe.wait_ge(exp_done, n * NBT + i - 1)
                score(2 * (i % 2), h0, nh, w, lambda h: k_b[:, h // 2, h % 2, kb * P:(kb + 1) * P],
                      lambda h: q_b[:, h // 2, q0:q0 + w], 0 if diagonal else None, mask_k).then_inc(b_scored, 1)

            def weigh(n, s):
                qc, kb = B_STEPS[s]
                w = span_b(qc, kb)[1]
                tiles = max(i for i, t in enumerate(B_TILES) if t[0] == s) + 1
                pe.wait_ge(exp_done, n * NBT + tiles)
                if kb == 0 and qc:
                    pe.wait_ge(raw_copied, n * CHUNKS + qc)
                for g in range(G):
                    mm = nc.tensor.matmul(ps[SLOT * g:SLOT * g + VW, 6, CH - w:CH], v_b[:, kb, g, :],
                                          probs[:, s % SLOTS, g, 0:w], start=(kb == 0), stop=(s == LAST_STEP[qc]))
                mm.then_inc(pv_done, 1)

            def turn_max(n):
                pe.wait_ge(m_step, n * M_STEPS + M_STEPS)
                nc.tensor.transpose(ps[0:M_COLS, 6, 0:P // 2].bitcast(BF16),
                                    m_parts[:, :, :, :, :].rearrange("p c r a q -> p (c r a q)"),
                                    ident_h[:, :]).then_inc(m_turned, 1)

            def phase_1(n, first):
                order = phase_1_order(first)
                turn_at = order.index(("maxima", 0)) + 2
                for at, (what, i) in enumerate(order):
                    if what == "max":
                        if i >= (0 if first else HOSTED) + 2:
                            pe.wait_ge(a_reduced, n * NA + i - 1)
                        score_a(n, i, 2 * (i % 2))
                    elif what == "ffn":
                        if i == 12:
                            pe.wait_ge(a_reduced, n * NA + NA)
                        if first and i == 0:
                            pe.wait_ge(w_lo_ready, 2)
                        if first or i >= B_LAG:
                            gate_up(n, i)
                        if first and i == LAG:
                            pe.wait_ge(w_lo_ready, 3)
                        if not first and i == LAG:
                            pe.wait_ge(silu_step, n * SILU_STEPS)
                        if i >= LAG:
                            down(n, i - LAG)
                    if at == turn_at:
                        turn_max(n)

            def phase_2(n, beside, closing=None):
                down(n, NC - LAG)
                pe.wait_ge(b_loaded, n * 80 + 80)
                pe.wait_ge(m_loaded, n * 32 + 32)
                tile = 0
                for s in range(NB):
                    while tile < NBT and B_TILES[tile][0] == s:
                        score_b(n, tile)
                        if s == 0:
                            down(n, NC - LAG + 1 + tile)
                        tile += 1
                    if s >= B_LAG:
                        weigh(n, s - B_LAG)
                    beside(s)
                for i in range(B_LAG):
                    weigh(n, NB - B_LAG + i)
                for i in range(B_LAG if closing else 0):
                    closing(i)

            def hosted(following):
                def beside(s):
                    if s == 0:
                        pe.wait_ge(a_loaded, following * 64 + 64)
                    if s < HOSTED:
                        if s >= 1:
                            pe.wait_ge(a_reduced, following * NA + s)
                        score_a(following, s, 4)
                return beside

            def first_steps(following):
                def closing(i):
                    if i == 0:
                        pe.wait_ge(a_reduced, following * NA + HOSTED)
                    gate_up(following, i)
                return closing

            def project(c):
                pe.wait_ge(ctxt_ready, c + 1)
                if c == B * CHUNKS - 1:
                    pe.wait_ge(others_divided, 1)
                if c == 0:
                    pe.wait_ge(out_loaded, 32)
                nc.tensor.matmul(ps[:, 4, :], w_out_sb[:, :], ctx_in[c], start=True, stop=True)\
                  .then_inc(proj_done, 1)

            def turn_y(c):
                pe.wait_ge(y_ready, c + 1)
                if c >= 1:
                    pe.wait_ge(o_ready, c)
                for t in range(4):
                    mm = nc.tensor.transpose(ps[:, 5, t * P:(t + 1) * P], y_t[:, t * P:(t + 1) * P], ident[:, :])
                mm.then_inc(y_turned, 1)

            pe.wait_ge(rest_ready, 4 * B)
            pe.wait_ge(a_loaded, 64)
            phase_1(0, True)
            pe.wait_ge(ones_placed, 32)
            with pe.Fori(1, UNITS) as n:
                phase_2(n - 1, hosted(n), first_steps(n))
                phase_1(n, False)
            output = {4: (project, 0), 7: (turn_y, 0), 8: (project, 1), 11: (turn_y, 1)}

            def output_beside(s):
                if s in output:
                    step, c = output[s]
                    step(c)

            phase_2(UNITS - 1, output_beside)
            project(2)
            pe.wait_ge(raw_copied, UNITS * CHUNKS)
            pe.wait_ge(silu_step, UNITS * SILU_STEPS)
            for t in range(4):
                mm = nc.tensor.transpose(ps[:, 7, t * P:(t + 1) * P], raw_t[:, t * P:(t + 1) * P], ident[:, :])
            mm.then_inc(tail_turned, 1)
            turn_y(2)
            pe.wait_ge(tail_step, 2)
            for t in range(4):
                mm = nc.tensor.transpose(ps[:, 6, t * P:(t + 1) * P], ctx_q[:, t, :], ident[:, :])
            mm.then_inc(tail_turned, 1)
            project(3)
            turn_y(3)


def kernel(L0_attn_x, L0_attn_in_proj_w, L0_attn_in_proj_b, L0_attn_out_proj_w, L0_attn_out_proj_b,
           L0_ffn_Wr, L0_ffn_Wg, L0_ffn_Wu, L0_ffn_Wd):
    import numpy as np
    import concourse.bacc as bacc
    from concourse import mybir as mb
    from concourse.bass_utils import run_bass_kernel_spmd

    nc = bacc.Bacc("TRN2", target_bir_lowering=False, num_devices=1)
    b_in = np.ascontiguousarray(L0_attn_in_proj_b)
    arrays = {
        "x": np.ascontiguousarray(L0_attn_x),
        "w_in": np.ascontiguousarray(np.asarray(L0_attn_in_proj_w).T),
        "b_in": np.ascontiguousarray(b_in.reshape(3, -1).T),
        "b_in_row": b_in.reshape(1, -1),
        "w_out": np.ascontiguousarray(np.asarray(L0_attn_out_proj_w).T),
        "b_out": np.ascontiguousarray(L0_attn_out_proj_b).reshape(-1, 1),
        "w_router": np.ascontiguousarray(L0_ffn_Wr),
        "w_gate": np.ascontiguousarray(L0_ffn_Wg),
        "w_up": np.ascontiguousarray(L0_ffn_Wu),
        "w_down": np.ascontiguousarray(L0_ffn_Wd),
    }
    args = [nc.dram_tensor(n, a.shape, mb.dt.from_np(a.dtype), kind="ExternalInput").ap() for n, a in arrays.items()]
    out = nc.dram_tensor("out", (B, S, E), mb.dt.float32, kind="ExternalOutput").ap()
    build(nc, *args, out)
    r = run_bass_kernel_spmd(nc, [arrays], core_ids=[0])
    return r.results[0]["out"]
```
